# Optimizing a Trainium2 kernel written in Bass

```python
import numpy as np
import jax
import jax.numpy as jnp

def _softmax(x, axis=-1):
    return jax.nn.softmax(x, axis=axis)

def _gelu(x):
    return jax.nn.gelu(x, approximate=True)

def _silu(x):
    return jax.nn.silu(x)

def _sigmoid(x):
    return jax.nn.sigmoid(x)

def _layernorm(x, axis=-1, eps=1e-05):
    m = jnp.mean(x, axis=axis, keepdims=True)
    v = jnp.var(x, axis=axis, keepdims=True)
    return (x - m) / jnp.sqrt(v + eps)

def _scatter_add(tgt, idx, src, axis=0):
    return tgt.at[idx].add(src)

def _segment_sum(src, seg, n):
    return jax.ops.segment_sum(src, seg, n)
kernel_name = 'mk_cond_seq_d1_seqx_r4_7d0102'

def setup_inputs(seed: int=0):
    np.random.seed(seed)
    _w = jnp.asarray

    def _rec_inputs():
        import jax
        import jax.numpy as jnp
        _rk = jax.random.key(seed)
        x = -0.0002928 + 1 * jax.random.normal(jax.random.fold_in(_rk, 1), (16, 256, 256), jnp.float32)
        _lenS = 256 - jax.random.randint(jax.random.fold_in(_rk, 7), (16,), 0, max(1, 256 // 4) + 1, jnp.int32)
        _lenS2 = 256 - jax.random.randint(jax.random.fold_in(_rk, 8), (16,), 0, max(1, 256 // 4) + 1, jnp.int32)
        fside_SxS_0 = -1.39391e-07 + 0.0999914 * jax.random.normal(jax.random.fold_in(_rk, 12), (256, 256), jnp.float32)
        cond_1024 = 0.00786388 + 1.0143 * jax.random.normal(jax.random.fold_in(_rk, 13), (16, 256), jnp.float32)
        _validS = jnp.arange(256)[None, :] < _lenS[:, None]
        _validS2 = jnp.arange(256)[None, :] < _lenS2[:, None]
        _causal = jnp.tril(jnp.ones((256, 256), dtype=bool))
        mask_SxS_ff0 = jnp.where(jnp.ones((256, 256), dtype=bool), 0.0, -1000000000.0).astype(jnp.float32)
        mask_BxS_bf0 = jnp.logical_not(jnp.ones((16, 256), dtype=bool))
        return (x, fside_SxS_0, cond_1024, mask_SxS_ff0, mask_BxS_bf0)
    x, fside_SxS_0, cond_1024, mask_SxS_ff0, mask_BxS_bf0 = _rec_inputs()

    def _L0_cond_setup():
        import jax, jax.numpy as jnp
        import numpy as np
        NUM_HEADS = 16
        LN_EPS = 1e-05

        def _linear(x, W, b):
            return x @ W + b

        def _adaln(x, c, Wss, bss):
            mu = jnp.mean(x, axis=-1, keepdims=True)
            var = jnp.mean((x - mu) ** 2, axis=-1, keepdims=True)
            h = (x - mu) * jax.lax.rsqrt(var + LN_EPS)
            ss = _linear(jax.nn.silu(c), Wss, bss)
            s, sh = jnp.split(ss, 2, axis=-1)
            return (1.0 + s)[:, None, :] * h + sh[:, None, :]
        key = jax.random.key(seed)
        ks = jax.random.split(key, 16)
        B, L, H = (2, 512, 256)
        Dff = 4 * H
        sc = 0.02
        inp = {'x': jax.random.normal(ks[0], (B, L, H), jnp.float32), 'attn_mask': jnp.zeros((L, L), jnp.float32), 'attn_bias': jax.random.normal(ks[1], (L, L), jnp.float32) * 0.1, 't_vec': jax.random.normal(ks[2], (B, H), jnp.float32), 'key_padding_mask': jnp.zeros((B, L), jnp.bool_), 'Wqkv': jax.random.normal(ks[3], (H, 3 * H), jnp.float32) * sc, 'bqkv': jnp.zeros((3 * H,), jnp.float32), 'Wproj': jax.random.normal(ks[4], (H, H), jnp.float32) * sc, 'bproj': jnp.zeros((H,), jnp.float32), 'Wss1': jax.random.normal(ks[5], (H, 2 * H), jnp.float32) * sc, 'bss1': jnp.zeros((2 * H,), jnp.float32), 'Wss2': jax.random.normal(ks[6], (H, 2 * H), jnp.float32) * sc, 'bss2': jnp.zeros((2 * H,), jnp.float32), 'Wmlp1': jax.random.normal(ks[7], (H, Dff), jnp.float32) * sc, 'bmlp1': jnp.zeros((Dff,), jnp.float32), 'Wmlp2': jax.random.normal(ks[8], (Dff, H), jnp.float32) * sc, 'bmlp2': jnp.zeros((H,), jnp.float32)}
        return inp
    _L0_cond_all = _L0_cond_setup()
    _L0_cond_in = {k: v for k, v in _L0_cond_all.items() if k in ('Wqkv', 'bqkv', 'Wproj', 'bproj', 'Wss1', 'bss1', 'Wss2', 'bss2', 'Wmlp1', 'bmlp1', 'Wmlp2', 'bmlp2')}
    del _L0_cond_all
    return {'x': x, 'fside_SxS_0': fside_SxS_0, 'cond_1024': cond_1024, 'mask_SxS_ff0': mask_SxS_ff0, 'mask_BxS_bf0': mask_BxS_bf0, 'L0_cond_Wqkv': _L0_cond_in['Wqkv'], 'L0_cond_bqkv': _L0_cond_in['bqkv'], 'L0_cond_Wproj': _L0_cond_in['Wproj'], 'L0_cond_bproj': _L0_cond_in['bproj'], 'L0_cond_Wss1': _L0_cond_in['Wss1'], 'L0_cond_bss1': _L0_cond_in['bss1'], 'L0_cond_Wss2': _L0_cond_in['Wss2'], 'L0_cond_bss2': _L0_cond_in['bss2'], 'L0_cond_Wmlp1': _L0_cond_in['Wmlp1'], 'L0_cond_bmlp1': _L0_cond_in['bmlp1'], 'L0_cond_Wmlp2': _L0_cond_in['Wmlp2'], 'L0_cond_bmlp2': _L0_cond_in['bmlp2']}

def reference(x, fside_SxS_0, cond_1024, mask_SxS_ff0, mask_BxS_bf0, L0_cond_Wqkv, L0_cond_bqkv, L0_cond_Wproj, L0_cond_bproj, L0_cond_Wss1, L0_cond_bss1, L0_cond_Wss2, L0_cond_bss2, L0_cond_Wmlp1, L0_cond_bmlp1, L0_cond_Wmlp2, L0_cond_bmlp2):
    import jax
    import jax.numpy as jnp

    def _L0_cond_ref(x, attn_mask, attn_bias, t_vec, key_padding_mask, Wqkv, bqkv, Wproj, bproj, Wss1, bss1, Wss2, bss2, Wmlp1, bmlp1, Wmlp2, bmlp2):
        import jax, jax.numpy as jnp
        import numpy as np
        NUM_HEADS = 16
        LN_EPS = 1e-05

        def _linear(x, W, b):
            return x @ W + b

        def _adaln(x, c, Wss, bss):
            mu = jnp.mean(x, axis=-1, keepdims=True)
            var = jnp.mean((x - mu) ** 2, axis=-1, keepdims=True)
            h = (x - mu) * jax.lax.rsqrt(var + LN_EPS)
            ss = _linear(jax.nn.silu(c), Wss, bss)
            s, sh = jnp.split(ss, 2, axis=-1)
            return (1.0 + s)[:, None, :] * h + sh[:, None, :]
        B, L, H = x.shape
        nh = NUM_HEADS
        hd = H // nh
        h = _adaln(x, t_vec, Wss1, bss1)
        qkv = _linear(h, Wqkv, bqkv).reshape(B, L, 3, nh, hd)
        q = qkv[:, :, 0].transpose(0, 2, 1, 3)
        k = qkv[:, :, 1].transpose(0, 2, 1, 3)
        v = qkv[:, :, 2].transpose(0, 2, 1, 3)
        scores = jnp.einsum('bhqd,bhkd->bhqk', q, k) / jnp.sqrt(jnp.asarray(hd, x.dtype))
        scores = scores + attn_mask + attn_bias
        big_neg = jnp.finfo(scores.dtype).min
        scores = jnp.where(key_padding_mask[:, None, None, :], big_neg, scores)
        w = jax.nn.softmax(scores, axis=-1)
        attn_out = jnp.einsum('bhqk,bhkd->bhqd', w, v)
        attn_out = attn_out.transpose(0, 2, 1, 3).reshape(B, L, H)
        x = x + _linear(attn_out, Wproj, bproj)
        h2 = _adaln(x, t_vec, Wss2, bss2)
        m = _linear(jax.nn.gelu(_linear(h2, Wmlp1, bmlp1), approximate=False), Wmlp2, bmlp2)
        return x + m
    x = _L0_cond_ref(x, mask_SxS_ff0, fside_SxS_0, cond_1024, mask_BxS_bf0, L0_cond_Wqkv, L0_cond_bqkv, L0_cond_Wproj, L0_cond_bproj, L0_cond_Wss1, L0_cond_bss1, L0_cond_Wss2, L0_cond_bss2, L0_cond_Wmlp1, L0_cond_bmlp1, L0_cond_Wmlp2, L0_cond_bmlp2)
    return x

_drawn_inputs = setup_inputs


def setup_inputs(seed=0):
    import zlib

    import numpy as np

    out = dict(_drawn_inputs(seed))
    spreads = {'mask_SxS_ff0': (0.0, 2.0),
     'L0_cond_bqkv': (0.0, 0.1),
     'L0_cond_bproj': (0.0, 0.1),
     'L0_cond_bss1': (0.0, 0.798),
     'L0_cond_bss2': (0.0, 0.505),
     'L0_cond_bmlp1': (0.0, 0.1),
     'L0_cond_bmlp2': (0.0, 0.1)}
    factors = {'fside_SxS_0': 40.811, 'L0_cond_Wss1': 2.867}
    for name, (base, spread) in spreads.items():
        noise = np.random.default_rng([zlib.crc32(name.encode()), seed]).standard_normal(out[name].shape)
        drawn = base * np.exp(spread * noise) if base else spread * noise
        out[name] = jnp.asarray(drawn.astype(out[name].dtype))
    for name, factor in factors.items():
        out[name] = (out[name] * factor).astype(out[name].dtype)
    return out
```

```python
from contextlib import ExitStack

import concourse.bass as bass
from concourse import mybir

F32 = mybir.dt.float32
F32R = mybir.dt.float32r
U8 = mybir.dt.uint8
ALU = mybir.AluOpType
ACT = mybir.ActivationFunctionType

P = 128
LN_EPS = 1e-5
FLT_MAX = 3.4028234663852886e38


def wait(eng, sem, value):
    if isinstance(value, int) and value <= 0:
        return
    eng.wait_ge(sem, value)


def build_block(nc, x, attn_bias, cond, attn_mask, key_padding, w_qkv, b_qkv, w_proj, b_proj,
                w_ss1, b_ss1, w_ss2, b_ss2, w_mlp1, b_mlp1, w_mlp2, b_mlp2, out):
    B, S, H = x.shape
    NH = 16
    D = H // NH
    DFF = w_mlp1.shape[1]
    TT = S // P
    CT = H // P
    FT = DFF // P
    PAIRS = NH // 2
    GROUPS = NH // 4
    UNITS = PAIRS * 2
    ROWS = 96
    Q_LO, Q_HI, K_HI, K_LO = range(4)
    HALF = NH // 2
    SCALE = float(D) ** -0.5
    assert (S, H, D, TT, CT, FT) == (256, 256, 16, 2, 2, 8)

    parts = nc.dram_tensor("qk_parts", (B, 2, 4, HALF, D, S), F32, kind="Internal").ap()

    with ExitStack() as ctx:
        def sb(name, shape, dt=F32):
            return ctx.enter_context(nc.sbuf_tensor(name, shape, dt))

        def bank(name):
            return ctx.enter_context(nc.psum_tensor(name, [P, 2, S], F32))

        def sem(name):
            return ctx.enter_context(nc.semaphore(name))

        tokens = sb("tokens", [P, B, TT, H])
        wqkv_hi = sb("wqkv_hi", [P, CT, 3 * H], F32R)
        wqkv_lo = sb("wqkv_lo", [P, CT, 3 * H], F32R)
        wproj_hi = sb("wproj_hi", [P, CT, H], F32R)
        wproj_lo = sb("wproj_lo", [P, CT, H], F32R)
        w1_hi = sb("w1_hi", [P, CT, DFF], F32R)
        w1_lo = sb("w1_lo", [P, CT, DFF], F32R)
        w2_hi = sb("w2_hi", [P, FT, H], F32R)
        w2_lo = sb("w2_lo", [P, FT, H], F32R)
        ident = sb("ident", [P, P])
        mod = sb("mod", [P, 8, B])
        bias_cols = sb("bias_cols", [P, 20])
        b_qk_col, b_ss_col, b_1_col = bias_cols[:, 0:4], bias_cols[:, 4:12], bias_cols[:, 12:20]
        b_v_row = sb("b_v_row", [P, H])
        b_proj_row = sb("b_proj_row", [P, H])
        b_2_row = sb("b_2_row", [P, H])
        pad_keys = sb("pad_keys", [P, B, S], U8)
        base_bias = sb("base_bias", [P, TT, S])
        bias = sb("bias", [P, TT, S])
        ln_st = sb("ln_st", [P, TT, 6])
        ln_mv = sb("ln_mv", [P, TT, 2])
        ln_ve = sb("ln_ve", [P, TT])
        ln_rs = sb("ln_rs", [P, TT])
        minus_half = sb("minus_half", [P, TT])
        xhat = sb("xhat", [P, TT, H])
        hT = sb("hT", [P, CT, S])
        hT_hi = sb("hT_hi", [P, CT, S], F32R)
        hT_lo = sb("hT_lo", [P, CT, S], F32R)
        qk = sb("qk", [P, 4, CT, S], F32R)
        stack = sb("stack", [ROWS, 2, 2, HALF, S], F32R)
        v_next = sb("v_next", [P, TT, H])
        v_ones = sb("v_ones", [P, TT, NH, 32])
        shifted = sb("shifted", [P, 8, 2, S])
        row_max = sb("row_max", [P, UNITS, 2])
        probs_t = sb("probs_t", [P, 8, 2, S])
        attn_t = sb("attn_t", [P, GROUPS, S])
        inv_sum = sb("inv_sum", [P, TT, NH])
        attn = sb("attn", [P, TT, NH, D])
        attnT_hi = sb("attnT_hi", [P, CT, S], F32R)
        attnT_lo = sb("attnT_lo", [P, CT, S], F32R)
        gelu = shifted[:, 0:4].rearrange("p a b c -> p (a b) c")
        gelu_hi = sb("gelu_hi", [P, FT, S], F32R)
        gelu_lo = sb("gelu_lo", [P, FT, S], F32R)
        result = sb("result", [P, TT, H])
        bias_rows = attn_t[0:20, 3, 0:P]
        cnd, cnd_e, cnd_r = (attn_t[0:B, n] for n in range(3))
        siluT = sb("siluT", [P, CT, B])
        w1_raw = probs_t[:, 0:4].rearrange("p a b c -> p (a b c)").rearrange("p (t n) -> p t n", t=CT)
        w2_raw = probs_t[:, 4:8].rearrange("p a b c -> p (a b c)").rearrange("p (t n) -> p t n", t=FT)
        wss_raw = shifted[:, 0:4].rearrange("p a b c -> p (a b c)").rearrange("p (l t n) -> p l t n", l=2, t=CT)
        wqkv_raw = shifted[:, 4:7].rearrange("p a b c -> p (a b c)").rearrange("p (t n) -> p t n", t=CT)
        wproj_raw = shifted[:, 7].rearrange("p b c -> p (b c)").rearrange("p (t n) -> p t n", t=CT)

        scores_ps = [bank("scores_ps0"), bank("scores_ps1")]
        trans_ps = [bank("trans_ps0"), bank("trans_ps1")]
        attn_ps = [bank("attn_ps0"), bank("attn_ps1")]
        job_x = bank("job_x")
        job_y = bank("job_y")

        ld_cond, ld_wss, ld_qkv, ld_proj, ld_w1, ld_w2 = (sem(n) for n in (
            "ld_cond", "ld_wss", "ld_qkv", "ld_proj", "ld_w1", "ld_w2"))
        ld_rows, ld_cols, ld_bias, x_loaded = (sem(n) for n in (
            "ld_rows", "ld_cols", "ld_bias", "x_loaded"))
        cols_transposed, cols_ready = sem("cols_transposed"), sem("cols_ready")
        stack_zeroed, half_ready = sem("stack_zeroed"), sem("half_ready")
        ident_zero, ident_ready, consts_ready = sem("ident_zero"), sem("ident_ready"), sem("consts_ready")
        cond_exp, cond_chain, silu_ready = sem("cond_exp"), sem("cond_chain"), sem("silu_ready")
        silu_transposed, siluT_ready, mod_products, mod_sum, mod_ready = (sem(n) for n in (
            "silu_transposed", "siluT_ready", "mod_products", "mod_sum", "mod_ready"))
        wq_scaled, wqkv_rounded, wqkv_split = sem("wq_scaled"), sem("wqkv_rounded"), sem("wqkv_split")
        w_rounded, w_split = sem("w_rounded"), sem("w_split")
        base_ready, bias_ready, bq_scaled = sem("base_ready"), sem("bias_ready"), sem("bq_scaled")
        ln_stats, ln_moments, ln_var_eps, ln_rstd, xhat_ready = (sem(n) for n in (
            "ln_stats", "ln_moments", "ln_var_eps", "ln_rstd", "xhat_ready"))
        x_transposed, h_modulated, h_rounded, h_split = (sem(n) for n in (
            "x_transposed", "h_modulated", "h_rounded", "h_split"))
        q_products, k_products, v_products = sem("q_products"), sem("k_products"), sem("v_products")
        q_rounded, k_rounded, q_split, k_split = (sem(n) for n in (
            "q_rounded", "k_rounded", "q_split", "k_split"))
        v_evacuated, v_installed = sem("v_evacuated"), sem("v_installed")
        stack_loaded = [sem(f"stack_loaded{j}") for j in range(2)]
        q_saved, k_saved = sem("q_saved"), sem("k_saved")
        scores_ready, maxed, shift_done, transposed, exp_done, attended = (sem(n) for n in (
            "scores_ready", "maxed", "shift_done", "transposed", "exp_done", "attended"))
        attn_evacuated, o_transposed, sums_inverted, normalized = (sem(n) for n in (
            "attn_evacuated", "o_transposed", "sums_inverted", "normalized"))
        n_transposed, n_rounded, n_split = sem("n_transposed"), sem("n_rounded"), sem("n_split")
        proj_products, x_biased, x1_ready, x1_biased = (sem(n) for n in (
            "proj_products", "x_biased", "x1_ready", "x1_biased"))
        up_products, gelu_ready, gelu_rounded, gelu_split = (sem(n) for n in (
            "up_products", "gelu_ready", "gelu_rounded", "gelu_split"))
        down_products, result_ready, stored = sem("down_products"), sem("result_ready"), sem("stored")

        block = ctx.enter_context(nc.Block())

        @block.sync
        def _(sp):
            sp.dma_start(cnd, cond).then_inc(ld_cond, 16)
            x_view = x.rearrange("b (t p) c -> p b t c", p=P)
            out_view = out.rearrange("b (t p) c -> p b t c", p=P)

            def load_x(b):
                wait(sp, x_loaded, 16 * b)
                sp.nop(nofuse=True)
                sp.dma_start(tokens[:, bass.ds(b, 1)], x_view[:, bass.ds(b, 1)]).then_inc(x_loaded, 16)

            load_x(0)
            sp.dma_start(wqkv_raw, w_qkv.rearrange("(t p) n -> p t n", p=P)).then_inc(ld_qkv, 16)
            load_x(1)
            for layer, w in ((0, w_ss1), (1, w_ss2)):
                sp.dma_start(wss_raw[:, layer], w.rearrange("(t p) n -> p t n", p=P)).then_inc(ld_wss, 16)
            for t in range(TT):
                sp.dma_start(base_bias[:, t], attn_bias[t * P:(t + 1) * P, :]).then_inc(ld_bias, 16)
                sp.dma_start(bias[:, t], attn_mask[t * P:(t + 1) * P, :]).then_inc(ld_bias, 16)
            load_x(2)
            sp.dma_start(wproj_raw, w_proj.rearrange("(t p) n -> p t n", p=P)).then_inc(ld_proj, 16)
            sp.dma_start(w1_raw, w_mlp1.rearrange("(t p) n -> p t n", p=P)).then_inc(ld_w1, 16)
            sp.dma_start(w2_raw, w_mlp2.rearrange("(t p) n -> p t n", p=P)).then_inc(ld_w2, 16)

            def save_parts(b, x0, split, saved):
                sp.wait_ge(split, 2 * b + 2)
                sp.nop(nofuse=True)
                for j in range(2):
                    sp.dma_start(parts[bass.ds(b, 1), j, x0:x0 + 2].rearrange("o x h d n -> (h d) (o x) n"),
                                 qk[:, x0:x0 + 2, j].bitcast(F32)).then_inc(saved, 16)

            def load_stack(b, first=False):
                sp.wait_ge(q_saved, 32 * b + 32)
                sp.wait_ge(k_saved, 32 * b + 32)
                for j in range(2):
                    if not first:
                        sp.wait_ge(scores_ready, UNITS * (b - 1) + HALF * (j + 1))
                    sp.nop(nofuse=True)
                    for r, sides, x0, n in ((0, slice(0, 2), Q_HI, 2), (1, slice(0, 1), Q_HI, 1), (1, slice(1, 2), K_LO, 1),
                                            (2, slice(0, 1), Q_LO, 1), (2, slice(1, 2), K_HI, 1)):
                        src = parts[bass.ds(b, 1), j, x0:x0 + n].rearrange("o x h d n -> d (o x h) n")
                        sp.dma_start(stack[r * D:(r + 1) * D, j, sides].rearrange("d s h n -> d (s h) n").bitcast(F32),
                                     src).then_inc(stack_loaded[j], 16)

            def next_stack(b, first=False):
                save_parts(b, Q_LO, q_split, q_saved)
                save_parts(b, K_HI, k_split, k_saved)
                load_stack(b, first)

            sp.wait_ge(stack_zeroed, 1)
            next_stack(0, first=True)
            next_stack(1)
            load_x(3)
            with sp.Fori(1, B - 3) as b:
                next_stack(b + 1)
                load_x(b + 3)
            next_stack(B - 2)
            next_stack(B - 1)
            with sp.Fori(0, B) as c:
                sp.wait_ge(result_ready, c + 1)
                sp.nop(nofuse=True)
                sp.dma_start(out_view[:, bass.ds(c, 1)], result[:].rearrange("p (o t) c -> p o t c", o=1)).then_inc(stored, 16)
                sp.wait_ge(stored, 16 * c + 16)
                sp.nop(nofuse=True)

        @block.gpsimd
        def _(pool):
            pool.memset(ident[:], 0.0).then_inc(ident_zero, 1)
            pool.wait_ge(ident_zero, 1)
            pool.affine_select(out=ident[:], in_=ident[:], compare_op=ALU.not_equal, fill=1.0, base=0,
                               pattern=[[-1, P]], channel_multiplier=1).then_inc(ident_ready, 1)
            pool.memset(minus_half[:], -0.5).then_inc(half_ready, 1)
            pool.memset(stack[:].bitcast(F32), 0.0).then_inc(stack_zeroed, 1)
            pool.wait_ge(half_ready, 1)

            def rstd(i):
                pool.wait_ge(ln_var_eps, i + 1)
                wait(pool, xhat_ready, 2 * i)
                pool.tensor_tensor(ln_rs[:], ln_ve[:], minus_half[:], ALU.pow).then_inc(ln_rstd, 1)

            rstd(0)
            rstd(1)
            for n, (raw, hi, lo) in enumerate(((wproj_raw, wproj_hi, wproj_lo), (w1_raw, w1_hi, w1_lo),
                                               (w2_raw, w2_hi, w2_lo))):
                pool.wait_ge(w_rounded, n + 1)
                pool.tensor_tensor(lo[:], raw, hi[:].bitcast(F32), ALU.subtract).then_inc(w_split, 1)

            def add_b_proj(b):
                pool.wait_ge(xhat_ready, 2 * b + 2)
                xb = tokens[:, bass.ds(b, 1)].rearrange("p o t c -> p (o t) c")
                pool.tensor_tensor(xb, xb, b_proj_row[:].unsqueeze(1).to_broadcast([P, TT, H]),
                                   ALU.add).then_inc(x_biased, 1)

            def shift_unit(b, u):
                pool.wait_ge(maxed, 2 * (UNITS * b + u) + 2)
                s = shifted[:, u % 8]
                pool.tensor_tensor(s, s, row_max[:, u, :].unsqueeze(2).to_broadcast([P, 2, S]),
                                   ALU.subtract).then_inc(shift_done, 1)

            pool.wait_ge(ld_cols, 16 * 4)
            add_b_proj(0)
            add_b_proj(1)

            def batch(b, has_next2=True):
                for u in range(UNITS):
                    shift_unit(b, u)
                    if u == 3 and has_next2:
                        rstd(b + 2)
                    if u == 9 and has_next2:
                        add_b_proj(b + 2)

            batch(0)
            batch(1)
            with pool.Fori(2, B - 2) as b:
                batch(b)
            batch(B - 2, False)
            batch(B - 1, False)
            rstd(B)
            rstd(B + 1)

            def add_b_2(c):
                pool.wait_ge(xhat_ready, 2 * (B + c) + 2)
                xb = tokens[:, bass.ds(c, 1)].rearrange("p o t c -> p (o t) c")
                pool.tensor_tensor(xb, xb, b_2_row[:].unsqueeze(1).to_broadcast([P, TT, H]),
                                   ALU.add).then_inc(x1_biased, 1)

            with pool.Fori(0, B - 2) as c:
                add_b_2(c)
                rstd(B + c + 2)
            add_b_2(B - 2)
            add_b_2(B - 1)

        @block.scalar
        def _(act):
            for r0, n, src in ((0, 4, b_qkv[0:2 * H]), (4, 4, b_ss1), (8, 4, b_ss2), (12, FT, b_mlp1)):
                act.dma_start(bias_rows[r0:r0 + n], src.rearrange("(t p) -> t p", p=P)).then_inc(ld_rows, 16)
            for row, src in ((b_v_row, b_qkv[2 * H:3 * H]), (b_proj_row, b_proj), (b_2_row, b_mlp2)):
                act.dma_start(row[:], src.rearrange("(o n) -> o n", o=1).to_broadcast([P, H])).then_inc(ld_cols, 16)
            act.dma_start(pad_keys[:], key_padding.rearrange("(o b) n -> o b n", o=1).to_broadcast([P, B, S])).then_inc(ld_cols, 16)
            act.wait_ge(ld_cond, 16)
            act.activation(cnd_e, cnd, ACT.Exp, scale=-1.0).then_inc(cond_exp, 1)
            for raw, hi, ld in ((wproj_raw, wproj_hi, ld_proj), (w1_raw, w1_hi, ld_w1), (w2_raw, w2_hi, ld_w2)):
                act.wait_ge(ld, 16)
                act.activation(hi[:], raw, ACT.Copy).then_inc(w_rounded, 1)

            def modulate(i, b, layer, free):
                act.wait_ge(x_transposed, i + 1)
                wait(act, h_split, i)
                for t in range(CT):
                    act.activation(hT[:, t], job_y[:, t], ACT.Identity,
                                   scale=mod[:, 4 * layer + t, bass.ds(b, 1)],
                                   bias=mod[:, 4 * layer + CT + t, bass.ds(b, 1)]).then_inc(h_modulated, 1)

            def round_q(b):
                act.wait_ge(q_products, b + 1)
                wait(act, q_saved, 32 * b)
                for t in range(CT):
                    act.activation(qk[:, Q_HI, t], job_x[:, t], ACT.Identity,
                                   bias=b_qk_col[:, t:t + 1]).then_inc(q_rounded, 1)

            def round_k(b):
                act.wait_ge(k_products, b + 1)
                wait(act, k_saved, 32 * b)
                for t in range(CT):
                    act.activation(qk[:, K_HI, t], job_y[:, t], ACT.Identity,
                                   bias=b_qk_col[:, CT + t:CT + t + 1]).then_inc(k_rounded, 1)

            def exp_unit(b, p, kt):
                n = UNITS * b + 2 * p + kt
                act.wait_ge(transposed, n + 1)
                if kt == 0:
                    wait(act, attended, GROUPS * b + p // 2 - 1)
                act.activation(probs_t[:, 2 * (p % 4) + kt], trans_ps[kt][:], ACT.Exp).then_inc(exp_done, 1)

            def evacuate_attn(b, j):
                act.wait_ge(attended, GROUPS * b + 2 * j + 2)
                wait(act, o_transposed, 2 * b)
                act.activation(attn_t[:, 2 * j:2 * j + 2], attn_ps[j][:], ACT.Copy).then_inc(attn_evacuated, 1)

            def round_attn(b):
                act.wait_ge(n_transposed, b + 1)
                wait(act, proj_products, b)
                act.activation(attnT_hi[:], job_x[:], ACT.Copy).then_inc(n_rounded, 1)

            act.wait_ge(mod_ready, 1)
            act.wait_ge(ld_cols, 16 * 4)
            act.wait_ge(bq_scaled, 1)
            modulate(0, 0, 0, None)
            round_q(0)
            round_k(0)
            act.wait_ge(v_products, 1)
            modulate(1, 1, 0, None)
            act.wait_ge(w_split, 3)

            def batch(b, prev=True, cur=True, nxt=True, nxt2=True):
                for s in range(PAIRS):
                    for kt in range(2):
                        if s >= 3 and cur:
                            exp_unit(b, s - 3, kt)
                        if s < 3 and prev:
                            exp_unit(b - 1, s + 5, kt)
                    if s == 0 and nxt:
                        round_q(b + 1)
                    if s == 1 and nxt:
                        round_k(b + 1)
                    if s == 3 and prev:
                        evacuate_attn(b - 1, 1)
                    if s == 3 and nxt2:
                        act.wait_ge(v_products, b + 2)
                        modulate(b + 2, b + 2, 0, None)
                    if s == 5 and prev:
                        round_attn(b - 1)
                    if s == 7 and cur:
                        evacuate_attn(b, 0)

            batch(0, prev=False)
            batch(1)
            with act.Fori(2, B - 2) as b:
                batch(b)
            batch(B - 2, nxt2=False)
            batch(B - 1, nxt=False, nxt2=False)
            batch(B, cur=False, nxt=False, nxt2=False)

            def modulate2(c):
                wait(act, up_products, 4 * c)
                modulate(B + c, c, 1, None)

            def gelu_chunk(c):
                for j in range(4):
                    act.wait_ge(up_products, 4 * c + j + 1)
                    wait(act, gelu_split, 4 * (c - 1) + j + 1)
                    ps = (scores_ps + trans_ps)[j]
                    for k in range(2):
                        act.activation(gelu[:, 2 * j + k], ps[:, k], ACT.Gelu,
                                       bias=b_1_col[:, 2 * j + k:2 * j + k + 1]).then_inc(gelu_ready, 1)

            modulate2(0)
            gelu_chunk(0)
            with act.Fori(1, B) as c:
                modulate2(c)
                gelu_chunk(c)

        @block.vector
        def _(dve):
            dve.memset(v_ones[:], 1.0).then_inc(consts_ready, 1)
            dve.wait_ge(cond_exp, 1)
            dve.tensor_scalar(cnd_e, cnd_e, 1.0, None, ALU.add).then_inc(cond_chain, 1)
            dve.wait_ge(cond_chain, 1)
            dve.reciprocal(cnd_r, cnd_e).then_inc(cond_chain, 1)
            dve.wait_ge(cond_chain, 2)
            dve.tensor_tensor(cnd_e, cnd, cnd_r, ALU.mult).then_inc(silu_ready, 1)

            def tokens_of(b):
                return tokens[:, bass.ds(b, 1)].rearrange("p o t c -> p (o t) c")

            def ln_moments_of(i, b):
                for t in range(TT):
                    dve.bn_stats(ln_st[:, t], tokens_of(b)[:, t]).then_inc(ln_stats, 1)
                dve.wait_ge(ln_stats, 2 * i + 2)
                dve.nop(nofuse=True)
                for t in range(TT):
                    dve.bn_aggr(ln_mv[:, t], ln_st[:, t]).then_inc(ln_moments, 1)
                dve.wait_ge(ln_moments, 2 * i + 2)
                dve.tensor_scalar(ln_ve[:], ln_mv[:, :, 1], LN_EPS, None, ALU.add).then_inc(ln_var_eps, 1)

            def ln_normalize(i, b):
                dve.wait_ge(ln_rstd, i + 1)
                wait(dve, x_transposed, i)
                for t in range(TT):
                    dve.tensor_scalar(xhat[:, t], tokens_of(b)[:, t], ln_mv[:, t, 0:1], ln_rs[:, t:t + 1],
                                      ALU.subtract, ALU.mult).then_inc(xhat_ready, 1)

            dve.wait_ge(x_loaded, 16)
            ln_moments_of(0, 0)
            ln_normalize(0, 0)
            dve.wait_ge(ld_qkv, 16)
            dve.tensor_scalar(wqkv_raw[:, :, 0:H], wqkv_raw[:, :, 0:H], SCALE, None, ALU.mult).then_inc(wq_scaled, 1)
            dve.wait_ge(wq_scaled, 1)
            dve.tensor_copy(wqkv_hi[:], wqkv_raw).then_inc(wqkv_rounded, 1)
            dve.wait_ge(wqkv_rounded, 1)
            dve.tensor_tensor(wqkv_lo[:], wqkv_raw, wqkv_hi[:].bitcast(F32), ALU.subtract).then_inc(wqkv_split, 1)
            dve.wait_ge(cols_transposed, 1)
            dve.tensor_copy(bias_cols[:], job_y[:, 0, 0:20]).then_inc(cols_ready, 1)
            dve.wait_ge(cols_ready, 1)
            dve.tensor_scalar(bias_cols[:, 0:2], bias_cols[:, 0:2], SCALE, None, ALU.mult).then_inc(bq_scaled, 1)
            dve.wait_ge(silu_transposed, 1)
            dve.tensor_copy(siluT[:], job_x[:, :, 0:B]).then_inc(siluT_ready, 1)
            dve.wait_ge(mod_products, 1)
            dve.tensor_tensor(mod[:], job_x[:, 0, 0:8 * B].rearrange("p (m b) -> p m b", b=B),
                              b_ss_col.unsqueeze(2).to_broadcast([P, 8, B]), ALU.add).then_inc(mod_sum, 1)
            dve.wait_ge(mod_sum, 1)
            scales = mod[:].rearrange("p (l k t) b -> p l k (t b)", l=2, k=2)[:, :, 0]
            dve.tensor_scalar(scales, scales, 1.0, None, ALU.add).then_inc(mod_ready, 1)
            dve.wait_ge(x_loaded, 32)
            ln_moments_of(1, 1)
            ln_normalize(1, 1)
            dve.wait_ge(ld_bias, 16 * 4)
            dve.tensor_tensor(base_bias[:], bias[:], base_bias[:], ALU.add).then_inc(base_ready, 1)
            dve.wait_ge(base_ready, 1)

            def make_bias(b):
                wait(dve, maxed, 2 * UNITS * b)
                pad = pad_keys[:, bass.ds(b, 1)].to_broadcast([P, TT, S])
                dve.scalar_tensor_tensor(bias[:], pad, -FLT_MAX, base_bias[:], ALU.mult, ALU.add).then_inc(bias_ready, 1)

            def split_h(i):
                dve.wait_ge(h_modulated, 2 * i + 2)
                dve.tensor_copy(hT_hi[:], hT[:]).then_inc(h_rounded, 1)
                dve.wait_ge(h_rounded, i + 1)
                dve.tensor_tensor(hT_lo[:], hT[:], hT_hi[:].bitcast(F32), ALU.subtract).then_inc(h_split, 1)

            def split_qk(b, hi, lo, ps, cols, rounded, split):
                dve.wait_ge(rounded, 2 * b + 2)
                for t in range(CT):
                    dve.scalar_tensor_tensor(qk[:, lo, t], ps[:, t], cols[:, t:t + 1],
                                             qk[:, hi, t].bitcast(F32), ALU.add, ALU.subtract).then_inc(split, 1)

            def split_q(b):
                split_qk(b, Q_HI, Q_LO, job_x, b_qk_col[:, 0:CT], q_rounded, q_split)

            def split_k(b):
                split_qk(b, K_HI, K_LO, job_y, b_qk_col[:, CT:2 * CT], k_rounded, k_split)

            def evacuate_v(b):
                dve.wait_ge(v_products, b + 1)
                wait(dve, v_installed, b)
                dve.tensor_tensor(v_next[:], job_x[:], b_v_row[:].unsqueeze(1).to_broadcast([P, TT, H]),
                                  ALU.add).then_inc(v_evacuated, 1)

            def install_v(b):
                dve.wait_ge(v_evacuated, b + 1)
                wait(dve, attended, GROUPS * b)
                dve.tensor_copy(v_ones[:, :, :, 0:D], v_next[:].rearrange("p t (h d) -> p t h d", d=D)).then_inc(v_installed, 1)

            def bias_and_max(b, u):
                n = UNITS * b + u
                p, qt = u // 2, u % 2
                dve.wait_ge(scores_ready, n + 1)
                if qt == 0:
                    wait(dve, transposed, n - 6)
                dve.nop(nofuse=True)
                for k in range(2):
                    dve.tensor_tensor_reduce(out=shifted[:, u % 8, k], in0=scores_ps[qt][:, k], in1=bias[:, qt],
                                             scale=1.0, scalar=-FLT_MAX, op0=ALU.add, op1=ALU.max,
                                             accum_out=row_max[:, u, k:k + 1]).then_inc(maxed, 1)

            def normalize(b, qt):
                ps = (job_x, job_y)[qt][:].rearrange("p a b -> p (a b)").rearrange("p (h e) -> p h e", e=32)
                dve.wait_ge(o_transposed, 2 * b + qt + 1)
                dve.reciprocal(inv_sum[:, qt], ps[:, :, D]).then_inc(sums_inverted, 1)
                dve.wait_ge(sums_inverted, 2 * b + qt + 1)
                wait(dve, n_transposed, b)
                dve.tensor_tensor(attn[:, qt], ps[:, :, 0:D], inv_sum[:, qt].unsqueeze(2).to_broadcast([P, NH, D]),
                                  ALU.mult).then_inc(normalized, 1)

            def split_attn(b):
                dve.wait_ge(n_rounded, b + 1)
                dve.tensor_tensor(attnT_lo[:], job_x[:], attnT_hi[:].bitcast(F32), ALU.subtract).then_inc(n_split, 1)

            def first_residual(b):
                dve.wait_ge(proj_products, b + 1)
                dve.wait_ge(x_biased, b + 1)
                xb = tokens[:, bass.ds(b, 1)].rearrange("p o t c -> p (o t) c")
                dve.tensor_tensor(xb, job_y[:], xb, ALU.add).then_inc(x1_ready, 1)

            dve.wait_ge(ld_cols, 16 * 4)
            make_bias(0)
            split_h(0)
            split_q(0)
            split_k(0)
            evacuate_v(0)
            dve.wait_ge(v_products, 1)
            split_h(1)
            dve.wait_ge(w_split, 3)
            dve.wait_ge(mod_products, 1)
            dve.wait_ge(bias_ready, 1)

            def batch(b, prev=True, cur=True, nxt=True, nxt2=True):
                for s in range(PAIRS):
                    if cur:
                        bias_and_max(b, 2 * s)
                        bias_and_max(b, 2 * s + 1)
                    if s == 0 and nxt2:
                        dve.wait_ge(x_loaded, 16 * (b + 3))
                        ln_moments_of(b + 2, b + 2)
                    if s == 1 and nxt:
                        split_q(b + 1)
                    if s == 2 and nxt:
                        split_k(b + 1)
                    if s == 2 and nxt2:
                        ln_normalize(b + 2, b + 2)
                    if s == 3 and cur:
                        install_v(b)
                    if s == 3 and nxt:
                        evacuate_v(b + 1)
                    if s == 4 and prev:
                        normalize(b - 1, 0)
                        normalize(b - 1, 1)
                    if s == 5 and nxt2:
                        split_h(b + 2)
                    if s == 6 and prev:
                        split_attn(b - 1)
                    if s == 7 and nxt:
                        make_bias(b + 1)
                    if s == 7 and prev:
                        first_residual(b - 1)
                    if s == 7 and nxt:
                        dve.wait_ge(bias_ready, b + 2)

            batch(0, prev=False)
            batch(1)
            with dve.Fori(2, B - 2) as b:
                batch(b)
            batch(B - 2, nxt2=False)
            batch(B - 1, nxt=False, nxt2=False)
            batch(B, cur=False, nxt=False, nxt2=False)

            def split_gelu(c, j):
                dve.wait_ge(gelu_ready, 8 * c + 2 * j + 2)
                if j == 0:
                    wait(dve, down_products, c)
                part = slice(2 * j, 2 * j + 2)
                dve.tensor_copy(gelu_hi[:, part], gelu[:, part]).then_inc(gelu_rounded, 1)
                dve.wait_ge(gelu_rounded, 4 * c + j + 1)
                dve.tensor_tensor(gelu_lo[:, part], gelu[:, part], gelu_hi[:, part].bitcast(F32),
                                  ALU.subtract).then_inc(gelu_split, 1)

            def second_residual(c):
                dve.wait_ge(down_products, c + 1)
                dve.wait_ge(x1_biased, c + 1)
                wait(dve, stored, 16 * c)
                xb = tokens[:, bass.ds(c, 1)].rearrange("p o t c -> p (o t) c")
                dve.tensor_tensor(result[:], attn_ps[0][:], xb, ALU.add).then_inc(result_ready, 1)

            def mlp_chunk(c, prev=True, nxt=True, nxt2=True):
                if nxt:
                    split_h(B + c + 1)
                if nxt2:
                    ln_moments_of(B + c + 2, c + 2)
                for j in range(4):
                    split_gelu(c, j)
                    if j == 0 and prev:
                        second_residual(c - 1)
                if nxt2:
                    ln_normalize(B + c + 2, c + 2)

            dve.wait_ge(x1_ready, B)
            ln_moments_of(B, 0)
            ln_normalize(B, 0)
            ln_moments_of(B + 1, 1)
            ln_normalize(B + 1, 1)
            split_h(B)
            mlp_chunk(0, prev=False)
            mlp_chunk(1)
            with dve.Fori(2, B - 2) as c:
                mlp_chunk(c)
            mlp_chunk(B - 2, nxt2=False)
            mlp_chunk(B - 1, nxt=False, nxt2=False)
            second_residual(B - 1)

        @block.tensor
        def _(pe):
            def products(out, terms):
                last = None
                for n, (l_hi, l_lo, r_hi, r_lo) in enumerate(terms):
                    pe.matmul(out, l_hi, r_hi, start=(n == 0), stop=False)
                    pe.matmul(out, l_hi, r_lo, start=False, stop=False)
                    last = pe.matmul(out, l_lo, r_hi, start=False, stop=(n == len(terms) - 1))
                return last

            def transpose_x(i):
                pe.wait_ge(xhat_ready, 2 * i + 2)
                for t in range(TT):
                    for c in range(CT):
                        last = pe.transpose(job_y[:, c, t * P:(t + 1) * P], xhat[:, t, c * P:(c + 1) * P], ident[:])
                last.then_inc(x_transposed, 1)

            def qk_tiles(b, side, ps, done):
                for t in range(2):
                    cols = slice((2 * side + t) * P, (2 * side + t + 1) * P)
                    last = products(ps[:, t], [(wqkv_hi[:, c, cols], wqkv_lo[:, c, cols], hT_hi[:, c], hT_lo[:, c])
                                               for c in range(CT)])
                last.then_inc(done, 1)

            def q_tiles(b):
                pe.wait_ge(h_split, b + 1)
                wait(pe, v_evacuated, b)
                qk_tiles(b, 0, job_x, q_products)

            def k_tiles(b):
                pe.wait_ge(h_modulated, 2 * b + 2)
                qk_tiles(b, 1, job_y, k_products)

            def v_tiles(b):
                pe.wait_ge(q_split, 2 * b + 2)
                for t in range(TT):
                    rows = slice(t * P, (t + 1) * P)
                    last = products(job_x[:, t], [(hT_hi[:, c, rows], hT_lo[:, c, rows], wqkv_hi[:, c, 2 * H:3 * H],
                                                   wqkv_lo[:, c, 2 * H:3 * H]) for c in range(CT)])
                last.then_inc(v_products, 1)

            def scores(b, p, qt):
                n = UNITS * b + 2 * p + qt
                if qt == 0 and p % 4 == 0:
                    pe.wait_ge(stack_loaded[p // 4], 16 * 5 * (b + 1))
                wait(pe, maxed, 2 * (n - 1))
                for k in range(2):
                    h = 2 * p + k
                    last = pe.matmul(scores_ps[qt][:, k], stack[:, h // HALF, 0, h % HALF, qt * P:(qt + 1) * P],
                                     stack[:, h // HALF, 1, h % HALF],
                                     start=True, stop=True)
                last.then_inc(scores_ready, 1)

            def transpose_scores(b, p, kt):
                n = UNITS * b + 2 * p + kt
                if kt == 0:
                    pe.wait_ge(shift_done, n + 2)
                wait(pe, exp_done, n - 1)
                for k in range(2):
                    for qt in range(TT):
                        last = pe.transpose(trans_ps[kt][:, k, qt * P:(qt + 1) * P],
                                            shifted[:, 2 * (p % 4) + qt, k, kt * P:(kt + 1) * P], ident[:])
                last.then_inc(transposed, 1)

            def attend(b, g):
                pe.wait_ge(exp_done, UNITS * b + 4 * g + 4)
                if g == 0:
                    pe.wait_ge(v_installed, b + 1)
                if g % 2 == 0:
                    wait(pe, attn_evacuated, 2 * b - 1 + g // 2)
                for kt in range(2):
                    for k in range(4):
                        h = 4 * g + k
                        last = pe.matmul(attn_ps[g // 2][32 * k:32 * k + 32, g % 2], v_ones[:, kt, h, :],
                                         probs_t[:, 2 * ((h // 2) % 4) + kt, h % 2], start=(kt == 0), stop=(kt == 1),
                                         tile_position=(0, 32 * k))
                last.then_inc(attended, 1)

            def transpose_o(b, qt):
                if qt == 0:
                    pe.wait_ge(attn_evacuated, 2 * b + 2)
                    wait(pe, n_split, b)
                    wait(pe, x1_ready, b)
                for g in range(GROUPS):
                    last = pe.transpose((job_x, job_y)[qt][:, g // 2, (g % 2) * P:(g % 2 + 1) * P],
                                        attn_t[:, g, qt * P:(qt + 1) * P], ident[:])
                last.then_inc(o_transposed, 1)

            def transpose_attn(b):
                pe.wait_ge(normalized, 2 * b + 2)
                for t in range(TT):
                    for c in range(CT):
                        src = attn[:, t].rearrange("p h d -> p (h d)")[:, c * P:(c + 1) * P]
                        last = pe.transpose(job_x[:, c, t * P:(t + 1) * P], src, ident[:])
                last.then_inc(n_transposed, 1)

            def project(b):
                pe.wait_ge(n_split, b + 1)
                for t in range(TT):
                    rows = slice(t * P, (t + 1) * P)
                    last = products(job_y[:, t], [(attnT_hi[:, c, rows], attnT_lo[:, c, rows], wproj_hi[:, c],
                                                   wproj_lo[:, c]) for c in range(CT)])
                last.then_inc(proj_products, 1)

            pe.wait_ge(ident_ready, 1)
            pe.wait_ge(ld_rows, 16 * 4)
            pe.transpose(job_y[:, 0, 0:20], bias_rows, ident[0:20, 0:20]).then_inc(cols_transposed, 1)
            pe.wait_ge(silu_ready, 1)
            for c in range(CT):
                last = pe.transpose(job_x[:, c, 0:B], cnd_e[:, c * P:(c + 1) * P], ident[0:B, 0:B])
            last.then_inc(silu_transposed, 1)
            pe.wait_ge(siluT_ready, 1)
            pe.wait_ge(ld_wss, 32)
            for m in range(8):
                for c in range(CT):
                    last = pe.matmul(job_x[:, 0, m * B:(m + 1) * B],
                                     wss_raw[:, m // 4, c, (m % 4) * P:(m % 4 + 1) * P], siluT[:, c],
                                     start=(c == 0), stop=(c == CT - 1))
            last.then_inc(mod_products, 1)
            pe.wait_ge(cols_ready, 1)
            transpose_x(0)
            pe.wait_ge(wqkv_split, 1)
            pe.wait_ge(mod_sum, 1)
            q_tiles(0)
            k_tiles(0)
            v_tiles(0)
            pe.wait_ge(k_split, 2)
            transpose_x(1)
            pe.wait_ge(consts_ready, 1)

            def batch(b, prev=True, cur=True, nxt=True, nxt2=True):
                for s in range(PAIRS):
                    for half in range(2):
                        if cur:
                            scores(b, s, half)
                        if s >= 3 and cur:
                            transpose_scores(b, s - 3, half)
                        if s < 3 and prev:
                            transpose_scores(b - 1, s + 5, half)
                    if s == 1 and prev:
                        attend(b - 1, 2)
                    if s == 3 and prev:
                        attend(b - 1, 3)
                    if s == 5 and cur:
                        attend(b, 0)
                    if s == 7 and cur:
                        attend(b, 1)
                    if s == 0 and nxt:
                        q_tiles(b + 1)
                    if s == 1 and nxt:
                        k_tiles(b + 1)
                    if s == 2 and nxt:
                        v_tiles(b + 1)
                    if s == 3 and nxt2:
                        pe.wait_ge(k_split, 2 * b + 4)
                        transpose_x(b + 2)
                    if s == 4 and prev:
                        if nxt:
                            pe.wait_ge(v_evacuated, b + 2)
                        if nxt2:
                            pe.wait_ge(h_modulated, 2 * b + 6)
                        transpose_o(b - 1, 0)
                        transpose_o(b - 1, 1)
                    if s == 5 and prev:
                        transpose_attn(b - 1)
                    if s == 7 and prev:
                        project(b - 1)

            batch(0, prev=False)
            batch(1)
            with pe.Fori(2, B - 2) as b:
                batch(b)
            batch(B - 2, nxt2=False)
            batch(B - 1, nxt=False, nxt2=False)
            batch(B, cur=False, nxt=False, nxt2=False)

            up_ps = scores_ps + trans_ps

            def mlp_up(c):
                pe.wait_ge(h_split, B + c + 1)
                for j in range(4):
                    wait(pe, gelu_ready, 8 * (c - 1) + 2 * j + 2)
                    for k in range(2):
                        cols = slice((2 * j + k) * P, (2 * j + k + 1) * P)
                        last = products(up_ps[j][:, k], [(w1_hi[:, t, cols], w1_lo[:, t, cols], hT_hi[:, t], hT_lo[:, t])
                                                         for t in range(CT)])
                    last.then_inc(up_products, 1)

            def mlp_down(c):
                wait(pe, result_ready, c)
                for t in range(TT):
                    rows = slice(t * P, (t + 1) * P)
                    if t == 0:
                        pe.wait_ge(gelu_split, 4 * c + 4)
                    last = products(attn_ps[0][:, t], [(gelu_hi[:, f, rows], gelu_lo[:, f, rows], w2_hi[:, f], w2_lo[:, f])
                                                       for f in range(FT)])
                last.then_inc(down_products, 1)

            def transpose_x2(c):
                wait(pe, h_modulated, 2 * (B + c))
                transpose_x(B + c)

            pe.wait_ge(x1_ready, B)
            pe.wait_ge(w_split, 3)
            transpose_x2(0)
            mlp_up(0)
            transpose_x2(1)
            mlp_up(1)
            mlp_down(0)
            transpose_x2(2)
            with pe.Fori(2, B - 1) as c:
                mlp_up(c)
                mlp_down(c - 1)
                transpose_x2(c + 1)
            mlp_up(B - 1)
            mlp_down(B - 2)
            mlp_down(B - 1)


_INS = ['x', 'fside_SxS_0', 'cond_1024', 'mask_SxS_ff0', 'mask_BxS_bf0', 'L0_cond_Wqkv', 'L0_cond_bqkv',
        'L0_cond_Wproj', 'L0_cond_bproj', 'L0_cond_Wss1', 'L0_cond_bss1', 'L0_cond_Wss2', 'L0_cond_bss2',
        'L0_cond_Wmlp1', 'L0_cond_bmlp1', 'L0_cond_Wmlp2', 'L0_cond_bmlp2']


def kernel(**inputs):
    import numpy as _np
    import concourse.bacc as _bacc
    from concourse import mybir as _mybir
    from concourse.bass_utils import run_bass_kernel_spmd as _run

    nc = _bacc.Bacc("TRN2", target_bir_lowering=False, num_devices=1)
    arrays, args = {}, []
    for name in _INS:
        a = _np.ascontiguousarray(inputs[name])
        arrays[f"in_{name}_dram"] = a
        args.append(nc.dram_tensor(f"in_{name}_dram", a.shape, _mybir.dt.from_np(a.dtype), kind="ExternalInput").ap())
    shape = _np.asarray(inputs['x']).shape
    args.append(nc.dram_tensor("out_0_dram", shape, _mybir.dt.float32, kind="ExternalOutput").ap())
    build_block(nc, *args)
    r = _run(nc, [arrays], core_ids=[0])
    return r.results[0]["out_0_dram"]
```

```python
from contextlib import ExitStack

import concourse.bass as bass
from concourse import mybir

F32 = mybir.dt.float32
F32R = mybir.dt.float32r
U8 = mybir.dt.uint8
ALU = mybir.AluOpType
ACT = mybir.ActivationFunctionType

P = 128
LN_EPS = 1e-5
FLT_MAX = 3.4028234663852886e38


def wait(eng, sem, value):
    if isinstance(value, int) and value <= 0:
        return
    eng.wait_ge(sem, value)


def build_block(nc, x, attn_bias, cond, attn_mask, key_padding, w_qkv, b_qkv, w_proj, b_proj,
                w_ss1, b_ss1, w_ss2, b_ss2, w_mlp1, b_mlp1, w_mlp2, b_mlp2, out):
    B, S, H = x.shape
    NH = 16
    D = H // NH
    DFF = w_mlp1.shape[1]
    TT = S // P
    CT = H // P
    FT = DFF // P
    PAIRS = NH // 2
    GROUPS = NH // 4
    UNITS = PAIRS * 2
    ROWS = 96
    Q_LO, Q_HI, K_HI, K_LO = range(4)
    HALF = NH // 2
    SCALE = float(D) ** -0.5
    assert (S, H, D, TT, CT, FT) == (256, 256, 16, 2, 2, 8)

    parts = nc.dram_tensor("qk_parts", (B, 2, 4, HALF, D, S), F32, kind="Internal").ap()

    with ExitStack() as ctx:
        def sb(name, shape, dt=F32):
            return ctx.enter_context(nc.sbuf_tensor(name, shape, dt))

        def bank(name):
            return ctx.enter_context(nc.psum_tensor(name, [P, 2, S], F32))

        def sem(name):
            return ctx.enter_context(nc.semaphore(name))

        tokens = sb("tokens", [P, B, TT, H])
        wqkv_hi = sb("wqkv_hi", [P, CT, 3 * H], F32R)
        wqkv_lo = sb("wqkv_lo", [P, CT, 3 * H], F32R)
        wproj_hi = sb("wproj_hi", [P, CT, H], F32R)
        wproj_lo = sb("wproj_lo", [P, CT, H], F32R)
        w1_hi = sb("w1_hi", [P, CT, DFF], F32R)
        w1_lo = sb("w1_lo", [P, CT, DFF], F32R)
        w2_hi = sb("w2_hi", [P, FT, H], F32R)
        w2_lo = sb("w2_lo", [P, FT, H], F32R)
        ident = sb("ident", [P, P])
        mod = sb("mod", [P, 8, B])
        bias_cols = sb("bias_cols", [P, 20])
        b_qk_col, b_ss_col, b_1_col = bias_cols[:, 0:4], bias_cols[:, 4:12], bias_cols[:, 12:20]
        b_v_row = sb("b_v_row", [P, H])
        b_proj_row = sb("b_proj_row", [P, H])
        b_2_row = sb("b_2_row", [P, H])
        pad_keys = sb("pad_keys", [P, B, S], U8)
        base_bias = sb("base_bias", [P, TT, S])
        bias = sb("bias", [P, TT, S])
        ln_st = sb("ln_st", [P, TT, 6])
        ln_mv = sb("ln_mv", [P, TT, 2])
        ln_ve = sb("ln_ve", [P, TT])
        ln_rs = sb("ln_rs", [P, TT])
        minus_half = sb("minus_half", [P, TT])
        xhat = sb("xhat", [P, TT, H])
        hT = sb("hT", [P, CT, S])
        hT_hi = sb("hT_hi", [P, CT, S], F32R)
        hT_lo = sb("hT_lo", [P, CT, S], F32R)
        qk = sb("qk", [P, 4, CT, S], F32R)
        stack = sb("stack", [ROWS, 2, 2, HALF, S], F32R)
        v_next = sb("v_next", [P, TT, H])
        v_ones = sb("v_ones", [P, TT, NH, 32])
        shifted = sb("shifted", [P, 8, 2, S])
        row_max = sb("row_max", [P, UNITS, 2])
        probs_t = sb("probs_t", [P, 8, 2, S])
        attn_t = sb("attn_t", [P, GROUPS, S])
        inv_sum = sb("inv_sum", [P, TT, NH])
        attn = sb("attn", [P, TT, NH, D])
        attnT_hi = sb("attnT_hi", [P, CT, S], F32R)
        attnT_lo = sb("attnT_lo", [P, CT, S], F32R)
        gelu = shifted[:, 0:4].rearrange("p a b c -> p (a b) c")
        gelu_hi = sb("gelu_hi", [P, FT, S], F32R)
        gelu_lo = sb("gelu_lo", [P, FT, S], F32R)
        result = sb("result", [P, TT, H])
        bias_rows = attn_t[0:20, 3, 0:P]
        cnd, cnd_e, cnd_r = (attn_t[0:B, n] for n in range(3))
        siluT = sb("siluT", [P, CT, B])
        w1_raw = probs_t[:, 0:4].rearrange("p a b c -> p (a b c)").rearrange("p (t n) -> p t n", t=CT)
        w2_raw = probs_t[:, 4:8].rearrange("p a b c -> p (a b c)").rearrange("p (t n) -> p t n", t=FT)
        wss_raw = shifted[:, 0:4].rearrange("p a b c -> p (a b c)").rearrange("p (l t n) -> p l t n", l=2, t=CT)
        wqkv_raw = shifted[:, 4:7].rearrange("p a b c -> p (a b c)").rearrange("p (t n) -> p t n", t=CT)
        wproj_raw = shifted[:, 7].rearrange("p b c -> p (b c)").rearrange("p (t n) -> p t n", t=CT)

        scores_ps = [bank("scores_ps0"), bank("scores_ps1")]
        trans_ps = [bank("trans_ps0"), bank("trans_ps1")]
        attn_ps = [bank("attn_ps0"), bank("attn_ps1")]
        job_x = bank("job_x")
        job_y = bank("job_y")

        ld_cond, ld_wss1, ld_wss2, ld_qkv, ld_proj, ld_w1, ld_w2 = (sem(n) for n in (
            "ld_cond", "ld_wss1", "ld_wss2", "ld_qkv", "ld_proj", "ld_w1", "ld_w2"))
        ld_rows, ld_cols, ld_bias, x_loaded = (sem(n) for n in (
            "ld_rows", "ld_cols", "ld_bias", "x_loaded"))
        cols_transposed, cols_ready = sem("cols_transposed"), sem("cols_ready")
        stack_zeroed, half_ready = sem("stack_zeroed"), sem("half_ready")
        ident_zero, ident_ready, consts_ready = sem("ident_zero"), sem("ident_ready"), sem("consts_ready")
        cond_exp, cond_chain, silu_ready = sem("cond_exp"), sem("cond_chain"), sem("silu_ready")
        silu_transposed, siluT_ready, mod_products, mod_sum, mod_ready = (sem(n) for n in (
            "silu_transposed", "siluT_ready", "mod_products", "mod_sum", "mod_ready"))
        wq_scaled, wqkv_rounded, wqkv_split = sem("wq_scaled"), sem("wqkv_rounded"), sem("wqkv_split")
        w_rounded, w_split = sem("w_rounded"), sem("w_split")
        base_ready, bias_ready, bq_scaled = sem("base_ready"), sem("bias_ready"), sem("bq_scaled")
        ln_stats, ln_moments, ln_var_eps, ln_rstd, xhat_ready = (sem(n) for n in (
            "ln_stats", "ln_moments", "ln_var_eps", "ln_rstd", "xhat_ready"))
        x_transposed, h_modulated, h_rounded, h_split = (sem(n) for n in (
            "x_transposed", "h_modulated", "h_rounded", "h_split"))
        q_products, k_products, v_products = sem("q_products"), sem("k_products"), sem("v_products")
        q_rounded, k_rounded, q_split, k_split = (sem(n) for n in (
            "q_rounded", "k_rounded", "q_split", "k_split"))
        v_evacuated, v_installed = sem("v_evacuated"), sem("v_installed")
        stack_loaded = [sem(f"stack_loaded{j}") for j in range(2)]
        q_saved, k_saved = sem("q_saved"), sem("k_saved")
        scores_ready, maxed, shift_done, transposed, exp_done, attended = (sem(n) for n in (
            "scores_ready", "maxed", "shift_done", "transposed", "exp_done", "attended"))
        attn_evacuated, o_transposed, sums_inverted, normalized = (sem(n) for n in (
            "attn_evacuated", "o_transposed", "sums_inverted", "normalized"))
        n_transposed, n_rounded, n_split = sem("n_transposed"), sem("n_rounded"), sem("n_split")
        proj_products, x_biased, x1_ready, x1_biased = (sem(n) for n in (
            "proj_products", "x_biased", "x1_ready", "x1_biased"))
        up_products, gelu_ready, gelu_rounded, gelu_split = (sem(n) for n in (
            "up_products", "gelu_ready", "gelu_rounded", "gelu_split"))
        down_products, result_ready, stored = sem("down_products"), sem("result_ready"), sem("stored")

        block = ctx.enter_context(nc.Block())

        @block.sync
        def _(sp):
            x_view = x.rearrange("b (t p) c -> p b t c", p=P)
            out_view = out.rearrange("b (t p) c -> p b t c", p=P)

            def load_x(b):
                wait(sp, x_loaded, 16 * b)
                sp.nop(nofuse=True)
                sp.dma_start(tokens[:, bass.ds(b, 1)], x_view[:, bass.ds(b, 1)]).then_inc(x_loaded, 16)

            load_x(0)
            sp.dma_start(wqkv_raw, w_qkv.rearrange("(t p) n -> p t n", p=P)).then_inc(ld_qkv, 16)
            load_x(1)
            for t in range(TT):
                sp.dma_start(base_bias[:, t], attn_bias[t * P:(t + 1) * P, :]).then_inc(ld_bias, 16)
                sp.dma_start(bias[:, t], attn_mask[t * P:(t + 1) * P, :]).then_inc(ld_bias, 16)
            load_x(2)
            sp.dma_start(wproj_raw, w_proj.rearrange("(t p) n -> p t n", p=P)).then_inc(ld_proj, 16)
            sp.dma_start(w1_raw, w_mlp1.rearrange("(t p) n -> p t n", p=P)).then_inc(ld_w1, 16)
            sp.dma_start(w2_raw, w_mlp2.rearrange("(t p) n -> p t n", p=P)).then_inc(ld_w2, 16)

            def save_parts(b, x0, split, saved):
                sp.wait_ge(split, 2 * b + 2)
                sp.nop(nofuse=True)
                for j in range(2):
                    sp.dma_start(parts[bass.ds(b, 1), j, x0:x0 + 2].rearrange("o x h d n -> (h d) (o x) n"),
                                 qk[:, x0:x0 + 2, j].bitcast(F32)).then_inc(saved, 16)

            def load_stack(b, first=False):
                sp.wait_ge(q_saved, 32 * b + 32)
                sp.wait_ge(k_saved, 32 * b + 32)
                for j in range(2):
                    if not first:
                        sp.wait_ge(scores_ready, UNITS * (b - 1) + HALF * (j + 1))
                    sp.nop(nofuse=True)
                    for r, sides, x0, n in ((0, slice(0, 2), Q_HI, 2), (1, slice(0, 1), Q_HI, 1), (1, slice(1, 2), K_LO, 1),
                                            (2, slice(0, 1), Q_LO, 1), (2, slice(1, 2), K_HI, 1)):
                        src = parts[bass.ds(b, 1), j, x0:x0 + n].rearrange("o x h d n -> d (o x h) n")
                        sp.dma_start(stack[r * D:(r + 1) * D, j, sides].rearrange("d s h n -> d (s h) n").bitcast(F32),
                                     src).then_inc(stack_loaded[j], 16)

            def next_stack(b, first=False):
                save_parts(b, Q_LO, q_split, q_saved)
                save_parts(b, K_HI, k_split, k_saved)
                load_stack(b, first)

            sp.wait_ge(stack_zeroed, 1)
            next_stack(0, first=True)
            next_stack(1)
            load_x(3)
            with sp.Fori(1, B - 3) as b:
                next_stack(b + 1)
                load_x(b + 3)
            next_stack(B - 2)
            next_stack(B - 1)
            with sp.Fori(0, B) as c:
                sp.wait_ge(result_ready, c + 1)
                sp.nop(nofuse=True)
                sp.dma_start(out_view[:, bass.ds(c, 1)], result[:].rearrange("p (o t) c -> p o t c", o=1)).then_inc(stored, 16)
                sp.wait_ge(stored, 16 * c + 16)
                sp.nop(nofuse=True)

        @block.gpsimd
        def _(pool):
            pool.memset(ident[:], 0.0).then_inc(ident_zero, 1)
            pool.wait_ge(ident_zero, 1)
            pool.affine_select(out=ident[:], in_=ident[:], compare_op=ALU.not_equal, fill=1.0, base=0,
                               pattern=[[-1, P]], channel_multiplier=1).then_inc(ident_ready, 1)
            pool.memset(minus_half[:], -0.5).then_inc(half_ready, 1)
            pool.memset(stack[:].bitcast(F32), 0.0).then_inc(stack_zeroed, 1)
            pool.wait_ge(half_ready, 1)

            def rstd(i):
                pool.wait_ge(ln_var_eps, i + 1)
                wait(pool, xhat_ready, 2 * i)
                pool.tensor_tensor(ln_rs[:], ln_ve[:], minus_half[:], ALU.pow).then_inc(ln_rstd, 1)

            rstd(0)
            rstd(1)
            for n, (raw, hi, lo) in enumerate(((wproj_raw, wproj_hi, wproj_lo), (w1_raw, w1_hi, w1_lo),
                                               (w2_raw, w2_hi, w2_lo))):
                pool.wait_ge(w_rounded, n + 1)
                pool.tensor_tensor(lo[:], raw, hi[:].bitcast(F32), ALU.subtract).then_inc(w_split, 1)

            def add_b_proj(b):
                pool.wait_ge(xhat_ready, 2 * b + 2)
                xb = tokens[:, bass.ds(b, 1)].rearrange("p o t c -> p (o t) c")
                pool.tensor_tensor(xb, xb, b_proj_row[:].unsqueeze(1).to_broadcast([P, TT, H]),
                                   ALU.add).then_inc(x_biased, 1)

            def shift_unit(b, u):
                pool.wait_ge(maxed, 2 * (UNITS * b + u) + 2)
                s = shifted[:, u % 8]
                pool.tensor_tensor(s, s, row_max[:, u, :].unsqueeze(2).to_broadcast([P, 2, S]),
                                   ALU.subtract).then_inc(shift_done, 1)

            pool.wait_ge(ld_cols, 16 * 4)
            add_b_proj(0)
            add_b_proj(1)

            def add_b_2(c):
                pool.wait_ge(xhat_ready, 2 * (B + c) + 2)
                xb = tokens[:, bass.ds(c, 1)].rearrange("p o t c -> p (o t) c")
                pool.tensor_tensor(xb, xb, b_2_row[:].unsqueeze(1).to_broadcast([P, TT, H]),
                                   ALU.add).then_inc(x1_biased, 1)

            def batch(b, chunk=None):
                for u in range(UNITS):
                    shift_unit(b, u)
                    if u == 3:
                        rstd(b + 2)
                    if u == 9:
                        add_b_proj(b + 2) if chunk is None else add_b_2(chunk)

            batch(0)
            batch(1)
            with pool.Fori(2, B - 2) as b:
                batch(b)
            batch(B - 2, chunk=0)
            batch(B - 1, chunk=1)
            with pool.Fori(2, B) as c:
                rstd(B + c)
                add_b_2(c)

        @block.scalar
        def _(act):
            act.dma_start(cnd, cond).then_inc(ld_cond, 16)
            act.dma_start(wss_raw[:, 0], w_ss1.rearrange("(t p) n -> p t n", p=P)).then_inc(ld_wss1, 16)
            for r0, n, src in ((0, 4, b_qkv[0:2 * H]), (4, 4, b_ss1), (8, 4, b_ss2), (12, FT, b_mlp1)):
                act.dma_start(bias_rows[r0:r0 + n], src.rearrange("(t p) -> t p", p=P)).then_inc(ld_rows, 16)
            act.wait_ge(ld_cond, 16)
            act.activation(cnd_e, cnd, ACT.Exp, scale=-1.0).then_inc(cond_exp, 1)
            act.dma_start(wss_raw[:, 1], w_ss2.rearrange("(t p) n -> p t n", p=P)).then_inc(ld_wss2, 16)
            for row, src in ((b_v_row, b_qkv[2 * H:3 * H]), (b_proj_row, b_proj), (b_2_row, b_mlp2)):
                act.dma_start(row[:], src.rearrange("(o n) -> o n", o=1).to_broadcast([P, H])).then_inc(ld_cols, 16)
            act.dma_start(pad_keys[:], key_padding.rearrange("(o b) n -> o b n", o=1).to_broadcast([P, B, S])).then_inc(ld_cols, 16)
            def modulate(i, b, layer):
                act.wait_ge(x_transposed, i + 1)
                wait(act, h_split, i)
                for t in range(CT):
                    act.activation(hT[:, t], job_y[:, t], ACT.Identity,
                                   scale=mod[:, 4 * layer + t, bass.ds(b, 1)],
                                   bias=mod[:, 4 * layer + CT + t, bass.ds(b, 1)]).then_inc(h_modulated, 1)

            def round_q(b):
                act.wait_ge(q_products, b + 1)
                wait(act, q_saved, 32 * b)
                for t in range(CT):
                    act.activation(qk[:, Q_HI, t], job_x[:, t], ACT.Identity,
                                   bias=b_qk_col[:, t:t + 1]).then_inc(q_rounded, 1)

            def round_k(b):
                act.wait_ge(k_products, b + 1)
                wait(act, k_saved, 32 * b)
                for t in range(CT):
                    act.activation(qk[:, K_HI, t], job_y[:, t], ACT.Identity,
                                   bias=b_qk_col[:, CT + t:CT + t + 1]).then_inc(k_rounded, 1)

            def exp_unit(b, p, kt):
                n = UNITS * b + 2 * p + kt
                act.wait_ge(transposed, n + 1)
                if kt == 0:
                    wait(act, attended, GROUPS * b + p // 2 - 1)
                act.activation(probs_t[:, 2 * (p % 4) + kt], trans_ps[kt][:], ACT.Exp).then_inc(exp_done, 1)

            def evacuate_attn(b, j):
                act.wait_ge(attended, GROUPS * b + 2 * j + 2)
                wait(act, o_transposed, 2 * b)
                act.activation(attn_t[:, 2 * j:2 * j + 2], attn_ps[j][:], ACT.Copy).then_inc(attn_evacuated, 1)

            def round_attn(b):
                act.wait_ge(n_transposed, b + 1)
                wait(act, proj_products, b)
                act.activation(attnT_hi[:], job_x[:], ACT.Copy).then_inc(n_rounded, 1)

            act.wait_ge(mod_ready, 1)
            act.wait_ge(bq_scaled, 1)
            modulate(0, 0, 0)
            round_q(0)
            round_k(0)
            modulate(1, 1, 0)
            for raw, hi, ld in ((wproj_raw, wproj_hi, ld_proj), (w1_raw, w1_hi, ld_w1), (w2_raw, w2_hi, ld_w2)):
                act.wait_ge(ld, 16)
                act.activation(hi[:], raw, ACT.Copy).then_inc(w_rounded, 1)
            act.wait_ge(w_split, 3)

            def gelu_part(c, j):
                act.wait_ge(up_products, 4 * c + j + 1)
                wait(act, gelu_split, 4 * (c - 1) + j + 1)
                ps = (scores_ps + trans_ps)[j]
                for k in range(2):
                    act.activation(gelu[:, 2 * j + k], ps[:, k], ACT.Gelu,
                                   bias=b_1_col[:, 2 * j + k:2 * j + k + 1]).then_inc(gelu_ready, 1)

            def batch(b, prev=True, cur=True, nxt=True, nxt2=True, chunk=None):
                for s in range(PAIRS):
                    for kt in range(2):
                        if s >= 3 and cur:
                            exp_unit(b, s - 3, kt)
                        if s < 3 and prev:
                            exp_unit(b - 1, s + 5, kt)
                    if s == 0 and nxt:
                        round_q(b + 1)
                    if s == 1 and nxt:
                        round_k(b + 1)
                    if s == 3 and prev:
                        evacuate_attn(b - 1, 1)
                    if s == 3 and nxt2:
                        modulate(b + 2, b + 2, 0)
                    if s == 3 and chunk is not None:
                        modulate(B + chunk, chunk, 1)
                    if s == 5 and prev:
                        round_attn(b - 1)
                    if s == 7 and cur:
                        evacuate_attn(b, 0)

            batch(0, prev=False)
            batch(1)
            with act.Fori(2, B - 2) as b:
                batch(b)
            batch(B - 2, nxt2=False, chunk=0)
            batch(B - 1, nxt=False, nxt2=False, chunk=1)
            batch(B, cur=False, nxt=False, nxt2=False)

            for c in range(2):
                gelu_part(c, 0)
                gelu_part(c, 1)
                gelu_part(c, 2)
                gelu_part(c, 3)
                modulate(B + c + 2, c + 2, 1)
            with act.Fori(2, B - 2) as c:
                for j in range(4):
                    gelu_part(c, j)
                modulate(B + c + 2, c + 2, 1)
            for c in range(B - 2, B):
                for j in range(4):
                    gelu_part(c, j)

        @block.vector
        def _(dve):
            dve.memset(v_ones[:], 1.0).then_inc(consts_ready, 1)
            dve.wait_ge(cond_exp, 1)
            dve.tensor_scalar(cnd_e, cnd_e, 1.0, None, ALU.add).then_inc(cond_chain, 1)
            dve.wait_ge(cond_chain, 1)
            dve.reciprocal(cnd_r, cnd_e).then_inc(cond_chain, 1)
            dve.wait_ge(cond_chain, 2)
            dve.tensor_tensor(cnd_e, cnd, cnd_r, ALU.mult).then_inc(silu_ready, 1)

            def tokens_of(b):
                return tokens[:, bass.ds(b, 1)].rearrange("p o t c -> p (o t) c")

            def ln_moments_of(i, b):
                for t in range(TT):
                    dve.bn_stats(ln_st[:, t], tokens_of(b)[:, t]).then_inc(ln_stats, 1)
                dve.wait_ge(ln_stats, 2 * i + 2)
                dve.nop(nofuse=True)
                for t in range(TT):
                    dve.bn_aggr(ln_mv[:, t], ln_st[:, t]).then_inc(ln_moments, 1)
                dve.wait_ge(ln_moments, 2 * i + 2)
                dve.tensor_scalar(ln_ve[:], ln_mv[:, :, 1], LN_EPS, None, ALU.add).then_inc(ln_var_eps, 1)

            def ln_normalize(i, b):
                dve.wait_ge(ln_rstd, i + 1)
                wait(dve, x_transposed, i)
                for t in range(TT):
                    dve.tensor_scalar(xhat[:, t], tokens_of(b)[:, t], ln_mv[:, t, 0:1], ln_rs[:, t:t + 1],
                                      ALU.subtract, ALU.mult).then_inc(xhat_ready, 1)

            def split_h(i):
                dve.wait_ge(h_modulated, 2 * i + 2)
                dve.tensor_copy(hT_hi[:], hT[:]).then_inc(h_rounded, 1)
                dve.wait_ge(h_rounded, i + 1)
                dve.tensor_tensor(hT_lo[:], hT[:], hT_hi[:].bitcast(F32), ALU.subtract).then_inc(h_split, 1)

            dve.wait_ge(x_loaded, 16)
            ln_moments_of(0, 0)
            ln_normalize(0, 0)
            dve.wait_ge(silu_transposed, 1)
            dve.tensor_copy(siluT[:], job_x[:, :, 0:B]).then_inc(siluT_ready, 1)
            dve.wait_ge(ld_qkv, 16)
            dve.tensor_scalar(wqkv_raw[:, :, 0:H], wqkv_raw[:, :, 0:H], SCALE, None, ALU.mult).then_inc(wq_scaled, 1)
            dve.wait_ge(wq_scaled, 1)
            dve.tensor_copy(wqkv_hi[:], wqkv_raw).then_inc(wqkv_rounded, 1)
            dve.wait_ge(wqkv_rounded, 1)
            dve.tensor_tensor(wqkv_lo[:], wqkv_raw, wqkv_hi[:].bitcast(F32), ALU.subtract).then_inc(wqkv_split, 1)
            dve.wait_ge(cols_transposed, 1)
            dve.tensor_copy(bias_cols[:], job_y[:, 0, 0:20]).then_inc(cols_ready, 1)
            dve.wait_ge(cols_ready, 1)
            dve.tensor_scalar(bias_cols[:, 0:2], bias_cols[:, 0:2], SCALE, None, ALU.mult).then_inc(bq_scaled, 1)

            def add_mod_bias(layer):
                dve.wait_ge(mod_products, layer + 1)
                m = slice(4 * layer, 4 * layer + 4)
                dve.tensor_tensor(mod[:, m], job_x[:, 0, 0:4 * B].rearrange("p (m b) -> p m b", b=B),
                                  b_ss_col[:, m].unsqueeze(2).to_broadcast([P, 4, B]), ALU.add).then_inc(mod_sum, 1)
                dve.wait_ge(mod_sum, layer + 1)
                scales = mod[:, 4 * layer:4 * layer + CT]
                dve.tensor_scalar(scales, scales, 1.0, None, ALU.add).then_inc(mod_ready, 1)

            add_mod_bias(0)
            split_h(0)
            dve.wait_ge(x_loaded, 32)
            ln_moments_of(1, 1)
            ln_normalize(1, 1)
            dve.wait_ge(ld_bias, 16 * 4)
            dve.tensor_tensor(base_bias[:], bias[:], base_bias[:], ALU.add).then_inc(base_ready, 1)
            dve.wait_ge(base_ready, 1)

            def make_bias(b):
                wait(dve, maxed, 2 * UNITS * b)
                pad = pad_keys[:, bass.ds(b, 1)].to_broadcast([P, TT, S])
                dve.scalar_tensor_tensor(bias[:], pad, -FLT_MAX, base_bias[:], ALU.mult, ALU.add).then_inc(bias_ready, 1)

            def split_qk(b, hi, lo, ps, cols, rounded, split):
                dve.wait_ge(rounded, 2 * b + 2)
                for t in range(CT):
                    dve.scalar_tensor_tensor(qk[:, lo, t], ps[:, t], cols[:, t:t + 1],
                                             qk[:, hi, t].bitcast(F32), ALU.add, ALU.subtract).then_inc(split, 1)

            def split_q(b):
                split_qk(b, Q_HI, Q_LO, job_x, b_qk_col[:, 0:CT], q_rounded, q_split)

            def split_k(b):
                split_qk(b, K_HI, K_LO, job_y, b_qk_col[:, CT:2 * CT], k_rounded, k_split)

            def evacuate_v(b):
                dve.wait_ge(v_products, b + 1)
                wait(dve, v_installed, b)
                dve.tensor_tensor(v_next[:], job_x[:], b_v_row[:].unsqueeze(1).to_broadcast([P, TT, H]),
                                  ALU.add).then_inc(v_evacuated, 1)

            def install_v(b):
                dve.wait_ge(v_evacuated, b + 1)
                wait(dve, attended, GROUPS * b)
                dve.tensor_copy(v_ones[:, :, :, 0:D], v_next[:].rearrange("p t (h d) -> p t h d", d=D)).then_inc(v_installed, 1)

            def bias_and_max(b, u):
                n = UNITS * b + u
                p, qt = u // 2, u % 2
                dve.wait_ge(scores_ready, n + 1)
                if qt == 0:
                    wait(dve, transposed, n - 6)
                dve.nop(nofuse=True)
                for k in range(2):
                    dve.tensor_tensor_reduce(out=shifted[:, u % 8, k], in0=scores_ps[qt][:, k], in1=bias[:, qt],
                                             scale=1.0, scalar=-FLT_MAX, op0=ALU.add, op1=ALU.max,
                                             accum_out=row_max[:, u, k:k + 1]).then_inc(maxed, 1)

            def normalize(b, qt):
                ps = (job_x, job_y)[qt][:].rearrange("p a b -> p (a b)").rearrange("p (h e) -> p h e", e=32)
                dve.wait_ge(o_transposed, 2 * b + qt + 1)
                dve.reciprocal(inv_sum[:, qt], ps[:, :, D]).then_inc(sums_inverted, 1)
                dve.wait_ge(sums_inverted, 2 * b + qt + 1)
                wait(dve, n_transposed, b)
                dve.tensor_tensor(attn[:, qt], ps[:, :, 0:D], inv_sum[:, qt].unsqueeze(2).to_broadcast([P, NH, D]),
                                  ALU.mult).then_inc(normalized, 1)

            def split_attn(b):
                dve.wait_ge(n_rounded, b + 1)
                dve.tensor_tensor(attnT_lo[:], job_x[:], attnT_hi[:].bitcast(F32), ALU.subtract).then_inc(n_split, 1)

            def first_residual(b):
                dve.wait_ge(proj_products, b + 1)
                dve.wait_ge(x_biased, b + 1)
                xb = tokens[:, bass.ds(b, 1)].rearrange("p o t c -> p (o t) c")
                dve.tensor_tensor(xb, job_y[:], xb, ALU.add).then_inc(x1_ready, 1)

            split_q(0)
            split_k(0)
            dve.wait_ge(ld_cols, 16 * 4)
            make_bias(0)
            evacuate_v(0)
            dve.wait_ge(v_products, 1)
            split_h(1)
            add_mod_bias(1)
            dve.wait_ge(w_split, 3)
            dve.wait_ge(bias_ready, 1)

            def split_h2(c):
                wait(dve, up_products, 4 * c)
                split_h(B + c)

            def batch(b, prev=True, cur=True, nxt=True, nxt2=True, chunk=None):
                for s in range(PAIRS):
                    if cur:
                        bias_and_max(b, 2 * s)
                        bias_and_max(b, 2 * s + 1)
                    if s == 0 and nxt2:
                        dve.wait_ge(x_loaded, 16 * (b + 3))
                        ln_moments_of(b + 2, b + 2)
                    if s == 0 and chunk is not None:
                        dve.wait_ge(x1_ready, chunk + 1)
                        ln_moments_of(B + chunk, chunk)
                    if s == 1 and nxt:
                        split_q(b + 1)
                    if s == 2 and nxt:
                        split_k(b + 1)
                    if s == 2 and nxt2:
                        ln_normalize(b + 2, b + 2)
                    if s == 2 and chunk is not None:
                        ln_normalize(B + chunk, chunk)
                    if s == 3 and cur:
                        install_v(b)
                    if s == 3 and nxt:
                        evacuate_v(b + 1)
                    if s == 4 and prev:
                        normalize(b - 1, 0)
                        normalize(b - 1, 1)
                    if s == 5 and nxt2:
                        dve.wait_ge(v_products, b + 2)
                        split_h(b + 2)
                    if s == 5 and chunk == 0:
                        dve.wait_ge(v_products, B)
                        split_h(B)
                    if s == 6 and prev:
                        split_attn(b - 1)
                    if s == 6 and not cur:
                        split_h2(1)
                    if s == 7 and nxt:
                        make_bias(b + 1)
                    if s == 7 and prev:
                        first_residual(b - 1)
                    if s == 7 and nxt:
                        dve.wait_ge(bias_ready, b + 2)

            batch(0, prev=False)
            batch(1)
            with dve.Fori(2, B - 2) as b:
                batch(b)
            batch(B - 2, nxt2=False, chunk=0)
            batch(B - 1, nxt=False, nxt2=False, chunk=1)
            batch(B, cur=False, nxt=False, nxt2=False)

            def split_gelu(c, j):
                dve.wait_ge(gelu_ready, 8 * c + 2 * j + 2)
                if j == 0:
                    wait(dve, down_products, c)
                part = slice(2 * j, 2 * j + 2)
                dve.tensor_copy(gelu_hi[:, part], gelu[:, part]).then_inc(gelu_rounded, 1)
                dve.wait_ge(gelu_rounded, 4 * c + j + 1)
                dve.tensor_tensor(gelu_lo[:, part], gelu[:, part], gelu_hi[:, part].bitcast(F32),
                                  ALU.subtract).then_inc(gelu_split, 1)

            def second_residual(c):
                dve.wait_ge(down_products, c + 1)
                dve.wait_ge(x1_biased, c + 1)
                wait(dve, stored, 16 * c)
                xb = tokens[:, bass.ds(c, 1)].rearrange("p o t c -> p (o t) c")
                dve.tensor_tensor(result[:], attn_ps[0][:], xb, ALU.add).then_inc(result_ready, 1)

            def mlp_chunk(c, prev=True, nxt=True, nxt2=True):
                if nxt2:
                    ln_moments_of(B + c + 2, c + 2)
                if nxt and not (isinstance(c, int) and c == 0):
                    split_h2(c + 1)
                if nxt2:
                    ln_normalize(B + c + 2, c + 2)
                if prev:
                    second_residual(c - 1)
                for j in range(4):
                    split_gelu(c, j)

            mlp_chunk(0, prev=False)
            mlp_chunk(1)
            with dve.Fori(2, B - 2) as c:
                mlp_chunk(c)
            mlp_chunk(B - 2, nxt2=False)
            mlp_chunk(B - 1, nxt=False, nxt2=False)
            second_residual(B - 1)

        @block.tensor
        def _(pe):
            def products(out, terms):
                last = None
                for n, (l_hi, l_lo, r_hi, r_lo) in enumerate(terms):
                    pe.matmul(out, l_hi, r_hi, start=(n == 0), stop=False)
                    pe.matmul(out, l_hi, r_lo, start=False, stop=False)
                    last = pe.matmul(out, l_lo, r_hi, start=False, stop=(n == len(terms) - 1))
                return last

            def transpose_x(i):
                pe.wait_ge(xhat_ready, 2 * i + 2)
                for t in range(TT):
                    for c in range(CT):
                        last = pe.transpose(job_y[:, c, t * P:(t + 1) * P], xhat[:, t, c * P:(c + 1) * P], ident[:])
                last.then_inc(x_transposed, 1)

            def qk_tiles(b, side, ps, done):
                for t in range(2):
                    cols = slice((2 * side + t) * P, (2 * side + t + 1) * P)
                    last = products(ps[:, t], [(wqkv_hi[:, c, cols], wqkv_lo[:, c, cols], hT_hi[:, c], hT_lo[:, c])
                                               for c in range(CT)])
                last.then_inc(done, 1)

            def q_tiles(b):
                pe.wait_ge(h_split, b + 1)
                wait(pe, v_evacuated, b)
                qk_tiles(b, 0, job_x, q_products)

            def k_tiles(b):
                pe.wait_ge(h_modulated, 2 * b + 2)
                qk_tiles(b, 1, job_y, k_products)

            def v_tiles(b):
                pe.wait_ge(q_split, 2 * b + 2)
                for t in range(TT):
                    rows = slice(t * P, (t + 1) * P)
                    last = products(job_x[:, t], [(hT_hi[:, c, rows], hT_lo[:, c, rows], wqkv_hi[:, c, 2 * H:3 * H],
                                                   wqkv_lo[:, c, 2 * H:3 * H]) for c in range(CT)])
                last.then_inc(v_products, 1)

            def scores(b, p, qt):
                n = UNITS * b + 2 * p + qt
                if qt == 0 and p % 4 == 0:
                    pe.wait_ge(stack_loaded[p // 4], 16 * 5 * (b + 1))
                wait(pe, maxed, 2 * (n - 1))
                for k in range(2):
                    h = 2 * p + k
                    last = pe.matmul(scores_ps[qt][:, k], stack[:, h // HALF, 0, h % HALF, qt * P:(qt + 1) * P],
                                     stack[:, h // HALF, 1, h % HALF],
                                     start=True, stop=True)
                last.then_inc(scores_ready, 1)

            def transpose_scores(b, p, kt):
                n = UNITS * b + 2 * p + kt
                if kt == 0:
                    pe.wait_ge(shift_done, n + 2)
                wait(pe, exp_done, n - 1)
                for k in range(2):
                    for qt in range(TT):
                        last = pe.transpose(trans_ps[kt][:, k, qt * P:(qt + 1) * P],
                                            shifted[:, 2 * (p % 4) + qt, k, kt * P:(kt + 1) * P], ident[:])
                last.then_inc(transposed, 1)

            def attend(b, g):
                pe.wait_ge(exp_done, UNITS * b + 4 * g + 4)
                if g == 0:
                    pe.wait_ge(v_installed, b + 1)
                if g % 2 == 0:
                    wait(pe, attn_evacuated, 2 * b - 1 + g // 2)
                for kt in range(2):
                    for k in range(4):
                        h = 4 * g + k
                        last = pe.matmul(attn_ps[g // 2][32 * k:32 * k + 32, g % 2], v_ones[:, kt, h, :],
                                         probs_t[:, 2 * ((h // 2) % 4) + kt, h % 2], start=(kt == 0), stop=(kt == 1),
                                         tile_position=(0, 32 * k))
                last.then_inc(attended, 1)

            def transpose_o(b, qt):
                if qt == 0:
                    pe.wait_ge(attn_evacuated, 2 * b + 2)
                    wait(pe, n_split, b)
                    wait(pe, x1_ready, b)
                for g in range(GROUPS):
                    last = pe.transpose((job_x, job_y)[qt][:, g // 2, (g % 2) * P:(g % 2 + 1) * P],
                                        attn_t[:, g, qt * P:(qt + 1) * P], ident[:])
                last.then_inc(o_transposed, 1)

            def transpose_attn(b):
                pe.wait_ge(normalized, 2 * b + 2)
                for t in range(TT):
                    for c in range(CT):
                        src = attn[:, t].rearrange("p h d -> p (h d)")[:, c * P:(c + 1) * P]
                        last = pe.transpose(job_x[:, c, t * P:(t + 1) * P], src, ident[:])
                last.then_inc(n_transposed, 1)

            def project(b):
                pe.wait_ge(n_split, b + 1)
                for t in range(TT):
                    rows = slice(t * P, (t + 1) * P)
                    last = products(job_y[:, t], [(attnT_hi[:, c, rows], attnT_lo[:, c, rows], wproj_hi[:, c],
                                                   wproj_lo[:, c]) for c in range(CT)])
                last.then_inc(proj_products, 1)

            pe.wait_ge(ident_ready, 1)
            pe.wait_ge(ld_rows, 16 * 4)
            pe.transpose(job_y[:, 0, 0:20], bias_rows, ident[0:20, 0:20]).then_inc(cols_transposed, 1)
            pe.wait_ge(silu_ready, 1)
            for c in range(CT):
                last = pe.transpose(job_x[:, c, 0:B], cnd_e[:, c * P:(c + 1) * P], ident[0:B, 0:B])
            last.then_inc(silu_transposed, 1)
            pe.wait_ge(siluT_ready, 1)

            def modulation(layer, loaded):
                pe.wait_ge(loaded, 16)
                for m in range(4):
                    for c in range(CT):
                        last = pe.matmul(job_x[:, 0, m * B:(m + 1) * B], wss_raw[:, layer, c, m * P:(m + 1) * P],
                                         siluT[:, c], start=(c == 0), stop=(c == CT - 1))
                last.then_inc(mod_products, 1)

            modulation(0, ld_wss1)
            pe.wait_ge(cols_ready, 1)
            transpose_x(0)
            pe.wait_ge(wqkv_split, 1)
            pe.wait_ge(mod_sum, 1)
            q_tiles(0)
            k_tiles(0)
            v_tiles(0)
            pe.wait_ge(k_split, 2)
            transpose_x(1)
            pe.wait_ge(v_evacuated, 1)
            modulation(1, ld_wss2)
            pe.wait_ge(mod_sum, 2)
            pe.wait_ge(consts_ready, 1)

            up_ps = scores_ps + trans_ps

            def mlp_up_part(c, j):
                if j == 0:
                    pe.wait_ge(h_split, B + c + 1)
                wait(pe, gelu_ready, 8 * (c - 1) + 2 * j + 2)
                for k in range(2):
                    cols = slice((2 * j + k) * P, (2 * j + k + 1) * P)
                    last = products(up_ps[j][:, k], [(w1_hi[:, t, cols], w1_lo[:, t, cols], hT_hi[:, t], hT_lo[:, t])
                                                     for t in range(CT)])
                last.then_inc(up_products, 1)

            def batch(b, prev=True, cur=True, nxt=True, nxt2=True, chunk=None):
                for s in range(PAIRS):
                    for half in range(2):
                        if cur:
                            scores(b, s, half)
                        if s >= 3 and cur:
                            transpose_scores(b, s - 3, half)
                        if s < 3 and prev:
                            transpose_scores(b - 1, s + 5, half)
                    if s == 1 and prev:
                        attend(b - 1, 2)
                    if s == 3 and prev:
                        attend(b - 1, 3)
                    if s == 5 and cur:
                        attend(b, 0)
                    if s == 7 and cur:
                        attend(b, 1)
                    if s == 0 and nxt:
                        q_tiles(b + 1)
                    if s == 1 and nxt:
                        k_tiles(b + 1)
                    if s == 2 and nxt:
                        v_tiles(b + 1)
                    if s == 3 and nxt2:
                        pe.wait_ge(k_split, 2 * b + 4)
                        transpose_x(b + 2)
                    if s == 3 and chunk is not None:
                        if nxt:
                            pe.wait_ge(k_split, 2 * b + 4)
                        transpose_x(B + chunk)
                    if s == 4 and prev:
                        if nxt:
                            pe.wait_ge(v_evacuated, b + 2)
                        if nxt2 or chunk is not None:
                            pe.wait_ge(h_modulated, 2 * b + 6)
                        transpose_o(b - 1, 0)
                        transpose_o(b - 1, 1)
                    if s == 5 and prev:
                        transpose_attn(b - 1)
                    if s == 7 and prev:
                        project(b - 1)
                    if not cur:
                        if s == 0:
                            pe.wait_ge(maxed, 2 * UNITS * B)
                            pe.wait_ge(w_split, 3)
                            mlp_up_part(0, 0)
                        if s == 1:
                            mlp_up_part(0, 1)
                        if s == 3:
                            pe.wait_ge(exp_done, UNITS * B)
                            mlp_up_part(0, 2)
                        if s == 4:
                            mlp_up_part(0, 3)

            batch(0, prev=False)
            batch(1)
            with pe.Fori(2, B - 2) as b:
                batch(b)
            batch(B - 2, nxt2=False, chunk=0)
            batch(B - 1, nxt=False, nxt2=False, chunk=1)
            batch(B, cur=False, nxt=False, nxt2=False)

            def mlp_up(c):
                for j in range(4):
                    mlp_up_part(c, j)

            def mlp_down(c):
                wait(pe, result_ready, c)
                for t in range(TT):
                    rows = slice(t * P, (t + 1) * P)
                    if t == 0:
                        pe.wait_ge(gelu_split, 4 * c + 4)
                    last = products(attn_ps[0][:, t], [(gelu_hi[:, f, rows], gelu_lo[:, f, rows], w2_hi[:, f], w2_lo[:, f])
                                                       for f in range(FT)])
                last.then_inc(down_products, 1)

            def transpose_x2(c):
                wait(pe, h_modulated, 2 * (B + c))
                transpose_x(B + c)

            mlp_up(1)
            pe.wait_ge(x1_ready, B)
            transpose_x2(2)
            mlp_down(0)
            with pe.Fori(2, B - 1) as c:
                mlp_up(c)
                transpose_x2(c + 1)
                mlp_down(c - 1)
            mlp_up(B - 1)
            mlp_down(B - 2)
            mlp_down(B - 1)


_INS = ['x', 'fside_SxS_0', 'cond_1024', 'mask_SxS_ff0', 'mask_BxS_bf0', 'L0_cond_Wqkv', 'L0_cond_bqkv',
        'L0_cond_Wproj', 'L0_cond_bproj', 'L0_cond_Wss1', 'L0_cond_bss1', 'L0_cond_Wss2', 'L0_cond_bss2',
        'L0_cond_Wmlp1', 'L0_cond_bmlp1', 'L0_cond_Wmlp2', 'L0_cond_bmlp2']


def kernel(**inputs):
    import numpy as _np
    import concourse.bacc as _bacc
    from concourse import mybir as _mybir
    from concourse.bass_utils import run_bass_kernel_spmd as _run

    nc = _bacc.Bacc("TRN2", target_bir_lowering=False, num_devices=1)
    arrays, args = {}, []
    for name in _INS:
        a = _np.ascontiguousarray(inputs[name])
        arrays[f"in_{name}_dram"] = a
        args.append(nc.dram_tensor(f"in_{name}_dram", a.shape, _mybir.dt.from_np(a.dtype), kind="ExternalInput").ap())
    shape = _np.asarray(inputs['x']).shape
    args.append(nc.dram_tensor("out_0_dram", shape, _mybir.dt.float32, kind="ExternalOutput").ap())
    build_block(nc, *args)
    r = _run(nc, [arrays], core_ids=[0])
    return r.results[0]["out_0_dram"]
```

```python
from contextlib import ExitStack

import concourse.bass as bass
from concourse import mybir

F32 = mybir.dt.float32
F32R = mybir.dt.float32r
U8 = mybir.dt.uint8
ALU = mybir.AluOpType
ACT = mybir.ActivationFunctionType

P = 128
LN_EPS = 1e-5
FLT_MAX = 3.4028234663852886e38


def wait(eng, sem, value):
    if isinstance(value, int) and value <= 0:
        return
    eng.wait_ge(sem, value)


def build_block(nc, x, attn_bias, cond, attn_mask, key_padding, w_qkv, b_qkv, w_proj, b_proj,
                w_ss1, b_ss1, w_ss2, b_ss2, w_mlp1, b_mlp1, w_mlp2, b_mlp2, out):
    B, S, H = x.shape
    NH = 16
    D = H // NH
    DFF = w_mlp1.shape[1]
    TT = S // P
    CT = H // P
    FT = DFF // P
    PAIRS = NH // 2
    GROUPS = NH // 4
    UNITS = PAIRS * 2
    ROWS = 96
    Q_LO, Q_HI, K_HI, K_LO = range(4)
    HALF = NH // 2
    SCALE = float(D) ** -0.5
    assert (S, H, D, TT, CT, FT) == (256, 256, 16, 2, 2, 8)

    parts = nc.dram_tensor("qk_parts", (B, 2, 4, HALF, D, S), F32, kind="Internal").ap()

    with ExitStack() as ctx:
        def sb(name, shape, dt=F32):
            return ctx.enter_context(nc.sbuf_tensor(name, shape, dt))

        def bank(name):
            return ctx.enter_context(nc.psum_tensor(name, [P, 2, S], F32))

        def sem(name):
            return ctx.enter_context(nc.semaphore(name))

        tokens = sb("tokens", [P, B, TT, H])
        wqkv_hi = sb("wqkv_hi", [P, CT, 3 * H], F32R)
        wqkv_lo = sb("wqkv_lo", [P, CT, 3 * H], F32R)
        wproj_hi = sb("wproj_hi", [P, CT, H], F32R)
        wproj_lo = sb("wproj_lo", [P, CT, H], F32R)
        w1_hi = sb("w1_hi", [P, CT, DFF], F32R)
        w1_lo = sb("w1_lo", [P, CT, DFF], F32R)
        w2_hi = sb("w2_hi", [P, FT, H], F32R)
        w2_lo = sb("w2_lo", [P, FT, H], F32R)
        ident = sb("ident", [P, P])
        mod = sb("mod", [P, 8, B])
        bias_cols = sb("bias_cols", [P, 20])
        b_qk_col, b_ss_col, b_1_col = bias_cols[:, 0:4], bias_cols[:, 4:12], bias_cols[:, 12:20]
        b_v_row = sb("b_v_row", [P, H])
        b_proj_row = sb("b_proj_row", [P, H])
        b_2_row = sb("b_2_row", [P, H])
        pad_keys = sb("pad_keys", [P, B, S], U8)
        base_bias = sb("base_bias", [P, TT, S])
        bias = sb("bias", [P, TT, S])
        ln_st = sb("ln_st", [P, TT, 6])
        ln_mv = sb("ln_mv", [P, TT, 2])
        ln_ve = sb("ln_ve", [P, TT])
        ln_rs = sb("ln_rs", [P, TT])
        minus_half = sb("minus_half", [P, TT])
        xhat = sb("xhat", [P, TT, H])
        hT = sb("hT", [P, CT, S])
        hT_hi = sb("hT_hi", [P, CT, S], F32R)
        hT_lo = sb("hT_lo", [P, CT, S], F32R)
        qk = sb("qk", [P, 4, CT, S], F32R)
        stack_mem = sb("stack", [P, 2, 2, HALF, S], F32R)
        stack = stack_mem[0:ROWS]
        v_next = sb("v_next", [P, TT, H])
        v_ones = sb("v_ones", [P, TT, NH, 32])
        shifted = sb("shifted", [P, 8, 2, S])
        row_max = sb("row_max", [P, UNITS, 2])
        probs_t = sb("probs_t", [P, 8, 2, S])
        attn_t = sb("attn_t", [P, GROUPS, S])
        inv_sum = sb("inv_sum", [P, TT, NH])
        attn = sb("attn", [P, TT, NH, D])
        attnT_hi = sb("attnT_hi", [P, CT, S], F32R)
        attnT_lo = sb("attnT_lo", [P, CT, S], F32R)
        gelu = shifted[:, 0:4].rearrange("p a b c -> p (a b) c")
        gelu_hi = sb("gelu_hi", [P, FT, S], F32R)
        gelu_lo = sb("gelu_lo", [P, FT, S], F32R)
        last_gelu_hi, last_gelu_lo = stack_mem[:, 0, 0], stack_mem[:, 0, 1]
        result = sb("result", [P, TT, H])
        bias_rows = attn_t[0:20, 3, 0:P]
        cnd = attn_t[0:B, 0]
        sigmoid_den = sb("sigmoid_den", [P, CT, B])
        sigmoid = sb("sigmoid", [P, CT, B])
        siluT = sb("siluT", [P, CT, B])
        w1_raw = probs_t[:, 0:4].rearrange("p a b c -> p (a b c)").rearrange("p (t n) -> p t n", t=CT)
        w2_raw = result[:]
        wss_raw = shifted[:, 0:4].rearrange("p a b c -> p (a b c)").rearrange("p (l t n) -> p l t n", l=2, t=CT)
        wqkv_raw = shifted[:, 4:7].rearrange("p a b c -> p (a b c)").rearrange("p (t n) -> p t n", t=CT)

        wproj_raw = shifted[:, 7].rearrange("p b c -> p (b c)").rearrange("p (t n) -> p t n", t=CT)

        scores_ps = [bank("scores_ps0"), bank("scores_ps1")]
        trans_ps = [bank("trans_ps0"), bank("trans_ps1")]
        attn_ps = [bank("attn_ps0"), bank("attn_ps1")]
        job_x = bank("job_x")
        job_y = bank("job_y")
        last_down_ps = (attn_ps[1], job_x)

        ld_cond, ld_wss1, ld_wss2, ld_qkv, ld_proj, ld_w1, ld_w2 = (sem(n) for n in (
            "ld_cond", "ld_wss1", "ld_wss2", "ld_qkv", "ld_proj", "ld_w1", "ld_w2"))
        ld_rows, ld_cols, ld_bias, x_loaded = (sem(n) for n in (
            "ld_rows", "ld_cols", "ld_bias", "x_loaded"))
        cols_transposed, cols_ready = sem("cols_transposed"), sem("cols_ready")
        stack_zeroed, half_ready = sem("stack_zeroed"), sem("half_ready")
        ident_zero, ident_ready, consts_ready = sem("ident_zero"), sem("ident_ready"), sem("consts_ready")
        cond_exp, cond_chain = sem("cond_exp"), sem("cond_chain")
        cond_transposed, siluT_ready, mod_products, mod_sum, mod_ready = (sem(n) for n in (
            "cond_transposed", "siluT_ready", "mod_products", "mod_sum", "mod_ready"))
        wq_scaled, wqkv_rounded, wqkv_split = sem("wq_scaled"), sem("wqkv_rounded"), sem("wqkv_split")
        w_rounded, w_split = sem("w_rounded"), sem("w_split")
        base_ready, bias_ready, bq_scaled = sem("base_ready"), sem("bias_ready"), sem("bq_scaled")
        ln_stats, ln_moments, ln_var_eps, ln_rstd, xhat_ready = (sem(n) for n in (
            "ln_stats", "ln_moments", "ln_var_eps", "ln_rstd", "xhat_ready"))
        x_transposed, h_modulated, h_rounded, h_split = (sem(n) for n in (
            "x_transposed", "h_modulated", "h_rounded", "h_split"))
        first_products, q_products, k_products, v_products = sem("first_products"), sem("q_products"), sem("k_products"), sem("v_products")
        q_rounded, k_rounded, q_split, k_split = (sem(n) for n in (
            "q_rounded", "k_rounded", "q_split", "k_split"))
        v_evacuated, v_installed = sem("v_evacuated"), sem("v_installed")
        stack_loaded = [sem(f"stack_loaded{j}") for j in range(2)]
        parts_saved = [sem(f"parts_saved{j}") for j in range(2)]
        scores_ready, maxed, shift_done, transposed, exp_done, attended = (sem(n) for n in (
            "scores_ready", "maxed", "shift_done", "transposed", "exp_done", "attended"))
        attn_evacuated, o_transposed, sums_inverted, normalized = (sem(n) for n in (
            "attn_evacuated", "o_transposed", "sums_inverted", "normalized"))
        n_transposed, n_rounded, n_split = sem("n_transposed"), sem("n_rounded"), sem("n_split")
        proj_products, x_biased, x1_ready, x1_biased = (sem(n) for n in (
            "proj_products", "x_biased", "x1_ready", "x1_biased"))
        up_products, gelu_ready, gelu_rounded, gelu_split = (sem(n) for n in (
            "up_products", "gelu_ready", "gelu_rounded", "gelu_split"))
        down_products, result_ready, stored = sem("down_products"), sem("result_ready"), sem("stored")

        block = ctx.enter_context(nc.Block())

        @block.sync
        def _(sp):
            x_view = x.rearrange("b (t p) c -> p b t c", p=P)
            out_view = out.rearrange("b (t p) c -> p b t c", p=P)

            def load_x(b):
                wait(sp, x_loaded, 16 * b)
                sp.nop(nofuse=True)
                sp.dma_start(tokens[:, bass.ds(b, 1)], x_view[:, bass.ds(b, 1)]).then_inc(x_loaded, 16)

            load_x(0)
            sp.dma_start(wss_raw[:, 0], w_ss1.rearrange("(t p) n -> p t n", p=P)).then_inc(ld_wss1, 16)
            sp.dma_start(wqkv_raw, w_qkv.rearrange("(t p) n -> p t n", p=P)).then_inc(ld_qkv, 16)
            load_x(1)
            sp.dma_start(w1_raw, w_mlp1.rearrange("(t p) n -> p t n", p=P)).then_inc(ld_w1, 16)
            for t in range(TT):
                sp.dma_start(base_bias[:, t], attn_bias[t * P:(t + 1) * P, :]).then_inc(ld_bias, 16)
                sp.dma_start(bias[:, t], attn_mask[t * P:(t + 1) * P, :]).then_inc(ld_bias, 16)
            sp.dma_start(wproj_raw, w_proj.rearrange("(t p) n -> p t n", p=P)).then_inc(ld_proj, 16)
            load_x(2)

            def load_w2(n):
                if n:
                    sp.wait_ge(w_split, 3 + n)
                sp.dma_start(w2_raw, w_mlp2.rearrange("(t p) n -> p t n", p=P)[:, 2 * n:2 * n + 2]).then_inc(ld_w2, 16)

            load_w2(0)

            def save_parts(b, x0, j):
                sp.dma_start(parts[bass.ds(b, 1), j, x0:x0 + 2].rearrange("o x h d n -> (h d) (o x) n"),
                             qk[:, x0:x0 + 2, j].bitcast(F32)).then_inc(parts_saved[j], 16)

            def load_stack(b, first=False):
                for j in range(2):
                    sp.wait_ge(parts_saved[j], 32 * b + 32)
                    sp.nop(nofuse=True)
                    if not first:
                        sp.wait_ge(scores_ready, UNITS * (b - 1) + HALF * (j + 1))
                    sp.nop(nofuse=True)
                    for r, sides, x0, n in ((0, slice(0, 2), Q_HI, 2), (1, slice(0, 1), Q_HI, 1), (1, slice(1, 2), K_LO, 1),
                                            (2, slice(0, 1), Q_LO, 1), (2, slice(1, 2), K_HI, 1)):
                        src = parts[bass.ds(b, 1), j, x0:x0 + n].rearrange("o x h d n -> d (o x h) n")
                        sp.dma_start(stack[r * D:(r + 1) * D, j, sides].rearrange("d s h n -> d (s h) n").bitcast(F32),
                                     src).then_inc(stack_loaded[j], 16)

            def next_stack(b):
                for x0, split in ((Q_LO, q_split), (K_HI, k_split)):
                    sp.wait_ge(split, 2 * b + 2)
                    sp.nop(nofuse=True)
                    for j in range(2):
                        save_parts(b, x0, j)
                load_stack(b)

            for j in range(2):
                sp.wait_ge(q_split, j + 1)
                save_parts(0, Q_LO, j)
                sp.wait_ge(k_split, j + 1)
                save_parts(0, K_HI, j)
            sp.wait_ge(stack_zeroed, 1)
            load_stack(0, first=True)
            load_x(3)
            next_stack(1)
            load_w2(1)
            with sp.Fori(1, B - 3) as b:
                next_stack(b + 1)
                load_x(b + 3)
            load_w2(2)
            next_stack(B - 2)
            next_stack(B - 1)
            load_w2(3)
            with sp.Fori(0, B - 1) as c:
                sp.wait_ge(result_ready, c + 1)
                sp.nop(nofuse=True)
                sp.dma_start(out_view[:, bass.ds(c, 1)], result[:].rearrange("p (o t) c -> p o t c", o=1)).then_inc(stored, 16)
                sp.wait_ge(stored, 16 * c + 16)
                sp.nop(nofuse=True)
            for t in range(TT):
                sp.wait_ge(result_ready, B + t)
                sp.dma_start(out_view[:, B - 1, t], result[:, t]).then_inc(stored, 16)
            sp.wait_ge(stored, 16 * (B - 1 + TT))

        @block.gpsimd
        def _(pool):
            pool.memset(ident[:], 0.0).then_inc(ident_zero, 1)
            pool.wait_ge(ident_zero, 1)
            pool.affine_select(out=ident[:], in_=ident[:], compare_op=ALU.not_equal, fill=1.0, base=0,
                               pattern=[[-1, P]], channel_multiplier=1).then_inc(ident_ready, 1)
            pool.memset(minus_half[:], -0.5).then_inc(half_ready, 1)
            pool.wait_ge(half_ready, 1)

            def rstd(i):
                pool.wait_ge(ln_var_eps, i + 1)
                wait(pool, xhat_ready, 2 * i)
                pool.tensor_tensor(ln_rs[:], ln_ve[:], minus_half[:], ALU.pow).then_inc(ln_rstd, 1)

            def add_b_proj(b):
                pool.wait_ge(xhat_ready, 2 * b + 2)
                xb = tokens[:, bass.ds(b, 1)].rearrange("p o t c -> p (o t) c")
                pool.tensor_tensor(xb, xb, b_proj_row[:].unsqueeze(1).to_broadcast([P, TT, H]),
                                   ALU.add).then_inc(x_biased, 1)

            def shift_unit(b, u):
                pool.wait_ge(maxed, 2 * (UNITS * b + u) + 2)
                s = shifted[:, u % 8]
                pool.tensor_tensor(s, s, row_max[:, u, :].unsqueeze(2).to_broadcast([P, 2, S]),
                                   ALU.subtract).then_inc(shift_done, 1)

            rstd(0)
            pool.memset(stack.bitcast(F32), 0.0).then_inc(stack_zeroed, 1)

            def split_weights(n, raw, hi, lo):
                pool.wait_ge(w_rounded, n + 1)
                pool.tensor_tensor(lo, raw, hi.bitcast(F32), ALU.subtract).then_inc(w_split, 1)

            split_weights(0, w1_raw[:, 0], w1_hi[:, 0], w1_lo[:, 0])
            rstd(1)
            split_weights(1, w1_raw[:, 1], w1_hi[:, 1], w1_lo[:, 1])
            split_weights(2, wproj_raw, wproj_hi[:], wproj_lo[:])
            pool.wait_ge(ld_cols, 16 * 4)
            add_b_proj(0)
            add_b_proj(1)

            def add_b_2(c):
                pool.wait_ge(xhat_ready, 2 * (B + c) + 2)
                xb = tokens[:, bass.ds(c, 1)].rearrange("p o t c -> p (o t) c")
                pool.tensor_tensor(xb, xb, b_2_row[:].unsqueeze(1).to_broadcast([P, TT, H]),
                                   ALU.add).then_inc(x1_biased, 1)

            def batch(b, chunk=None, w2_part=None):
                for u in range(UNITS):
                    shift_unit(b, u)
                    if u == 13 and w2_part is not None:
                        f = slice(2 * w2_part, 2 * w2_part + 2)
                        split_weights(3 + w2_part, w2_raw, w2_hi[:, f], w2_lo[:, f])
                    if u == 3:
                        rstd(b + 2)
                    if u == 9:
                        add_b_proj(b + 2) if chunk is None else add_b_2(chunk)

            batch(0, w2_part=0)
            batch(1, w2_part=1)
            with pool.Fori(2, B - 2) as b:
                batch(b)
            batch(B - 2, chunk=0, w2_part=2)
            batch(B - 1, chunk=1, w2_part=3)
            with pool.Fori(2, B) as c:
                rstd(B + c)
                add_b_2(c)

        @block.scalar
        def _(act):
            act.dma_start(cnd, cond).then_inc(ld_cond, 16)
            for r0, n, src in ((0, 4, b_qkv[0:2 * H]), (4, 4, b_ss1), (8, 4, b_ss2), (12, FT, b_mlp1)):
                act.dma_start(bias_rows[r0:r0 + n], src.rearrange("(t p) -> t p", p=P)).then_inc(ld_rows, 16)
            act.wait_ge(cond_transposed, 1)
            act.activation(sigmoid_den[:], job_x[:, :, 0:B], ACT.Exp, scale=-1.0).then_inc(cond_exp, 1)
            act.dma_start(wss_raw[:, 1], w_ss2.rearrange("(t p) n -> p t n", p=P)).then_inc(ld_wss2, 16)
            for row, src in ((b_v_row, b_qkv[2 * H:3 * H]), (b_proj_row, b_proj), (b_2_row, b_mlp2)):
                act.dma_start(row[:], src.rearrange("(o n) -> o n", o=1).to_broadcast([P, H])).then_inc(ld_cols, 16)
            act.dma_start(pad_keys[:], key_padding.rearrange("(o b) n -> o b n", o=1).to_broadcast([P, B, S])).then_inc(ld_cols, 16)
            def modulate(i, b, layer):
                act.wait_ge(x_transposed, i + 1)
                wait(act, h_split, i)
                for t in range(CT):
                    act.activation(hT[:, t], job_y[:, t], ACT.Identity,
                                   scale=mod[:, 4 * layer + t, bass.ds(b, 1)],
                                   bias=mod[:, 4 * layer + CT + t, bass.ds(b, 1)]).then_inc(h_modulated, 1)

            def round_q(b):
                act.wait_ge(q_products, b + 1)
                for t in range(CT):
                    wait(act, parts_saved[t], 32 * b)
                    act.activation(qk[:, Q_HI, t], job_x[:, t], ACT.Identity,
                                   bias=b_qk_col[:, t:t + 1]).then_inc(q_rounded, 1)

            def round_k(b):
                act.wait_ge(k_products, b + 1)
                for t in range(CT):
                    wait(act, parts_saved[t], 32 * b)
                    act.activation(qk[:, K_HI, t], job_y[:, t], ACT.Identity,
                                   bias=b_qk_col[:, CT + t:CT + t + 1]).then_inc(k_rounded, 1)

            def exp_unit(b, p, kt):
                n = UNITS * b + 2 * p + kt
                act.wait_ge(transposed, n + 1)
                if kt == 0:
                    wait(act, attended, GROUPS * b + p // 2 - 1)
                act.activation(probs_t[:, 2 * (p % 4) + kt], trans_ps[kt][:], ACT.Exp).then_inc(exp_done, 1)

            def evacuate_attn(b, j):
                act.wait_ge(attended, GROUPS * b + 2 * j + 2)
                wait(act, o_transposed, 2 * b)
                act.activation(attn_t[:, 2 * j:2 * j + 2], attn_ps[j][:], ACT.Copy).then_inc(attn_evacuated, 1)

            def round_attn(b):
                act.wait_ge(n_transposed, b + 1)
                wait(act, proj_products, b)
                act.activation(attnT_hi[:], job_x[:], ACT.Copy).then_inc(n_rounded, 1)

            act.wait_ge(mod_ready, 1)
            act.wait_ge(bq_scaled, 1)
            def round_weights(raw, hi):
                act.activation(hi, raw, ACT.Copy).then_inc(w_rounded, 1)

            modulate(0, 0, 0)
            act.wait_ge(ld_w1, 16)
            for t in range(CT):
                round_weights(w1_raw[:, t], w1_hi[:, t])
            for t in range(CT):
                act.wait_ge(*((q_products, 1) if t == CT - 1 else (first_products, 1)))
                act.activation(qk[:, Q_HI, t], scores_ps[t][:, 0], ACT.Identity,
                               bias=b_qk_col[:, t:t + 1]).then_inc(q_rounded, 1)
                act.wait_ge(*((k_products, 1) if t == CT - 1 else (first_products, 2)))
                act.activation(qk[:, K_HI, t], trans_ps[t][:, 0], ACT.Identity,
                               bias=b_qk_col[:, CT + t:CT + t + 1]).then_inc(k_rounded, 1)
            modulate(1, 1, 0)
            act.wait_ge(ld_proj, 16)
            round_weights(wproj_raw, wproj_hi[:])
            round_q(1)
            round_k(1)
            act.wait_ge(w_split, 2)

            def gelu_part(c, j):
                act.wait_ge(up_products, 4 * c + j + 1)
                wait(act, gelu_split, 4 * (c - 1) + j + 1)
                ps = (scores_ps + trans_ps)[j]
                for k in range(2):
                    act.activation(gelu[:, 2 * j + k], ps[:, k], ACT.Gelu,
                                   bias=b_1_col[:, 2 * j + k:2 * j + k + 1]).then_inc(gelu_ready, 1)

            def batch(b, prev=True, cur=True, nxt=True, nxt2=True, chunk=None, qk=True, w2_part=None):
                for s in range(PAIRS):
                    for kt in range(2):
                        if s >= 3 and cur:
                            exp_unit(b, s - 3, kt)
                        if s < 3 and prev:
                            exp_unit(b - 1, s + 5, kt)
                    if s == 0 and nxt and qk:
                        round_q(b + 1)
                    if s == 1 and nxt and qk:
                        round_k(b + 1)
                    if s == 3 and prev:
                        evacuate_attn(b - 1, 1)
                    if s == 3 and not cur:
                        gelu_part(0, 0)
                        gelu_part(0, 1)
                        gelu_part(0, 2)
                    if s == 3 and nxt2:
                        modulate(b + 2, b + 2, 0)
                    if s == 3 and chunk is not None:
                        modulate(B + chunk, chunk, 1)
                    if s == 5 and prev:
                        round_attn(b - 1)
                    if s == 7 and cur:
                        evacuate_attn(b, 0)
                    if s == 6 and w2_part is not None:
                        act.wait_ge(ld_w2, 16 * (w2_part + 1))
                        round_weights(w2_raw, w2_hi[:, 2 * w2_part:2 * w2_part + 2])

            batch(0, prev=False, qk=False, w2_part=0)
            batch(1, w2_part=1)
            with act.Fori(2, B - 2) as b:
                batch(b)
            batch(B - 2, nxt2=False, chunk=0, w2_part=2)
            batch(B - 1, nxt=False, nxt2=False, chunk=1, w2_part=3)
            batch(B, cur=False, nxt=False, nxt2=False)

            gelu_part(0, 3)
            modulate(B + 2, 2, 1)
            for j in range(4):
                gelu_part(1, j)
            modulate(B + 3, 3, 1)
            with act.Fori(2, B - 2) as c:
                for j in range(4):
                    gelu_part(c, j)
                modulate(B + c + 2, c + 2, 1)
            for c in range(B - 2, B):
                for j in range(4):
                    gelu_part(c, j)

        @block.vector
        def _(dve):
            dve.memset(v_ones[:], 1.0).then_inc(consts_ready, 1)
            def tokens_of(b):
                return tokens[:, bass.ds(b, 1)].rearrange("p o t c -> p (o t) c")

            def ln_moments_of(i, b):
                for t in range(TT):
                    dve.bn_stats(ln_st[:, t], tokens_of(b)[:, t]).then_inc(ln_stats, 1)
                dve.wait_ge(ln_stats, 2 * i + 2)
                dve.nop(nofuse=True)
                for t in range(TT):
                    dve.bn_aggr(ln_mv[:, t], ln_st[:, t]).then_inc(ln_moments, 1)
                dve.wait_ge(ln_moments, 2 * i + 2)
                dve.tensor_scalar(ln_ve[:], ln_mv[:, :, 1], LN_EPS, None, ALU.add).then_inc(ln_var_eps, 1)

            def ln_normalize(i, b):
                dve.wait_ge(ln_rstd, i + 1)
                wait(dve, x_transposed, i)
                for t in range(TT):
                    dve.tensor_scalar(xhat[:, t], tokens_of(b)[:, t], ln_mv[:, t, 0:1], ln_rs[:, t:t + 1],
                                      ALU.subtract, ALU.mult).then_inc(xhat_ready, 1)

            def round_h(i):
                dve.wait_ge(h_modulated, 2 * i + 2)
                dve.tensor_copy(hT_hi[:], hT[:]).then_inc(h_rounded, 1)

            def split_h(i, rounded=False):
                if not rounded:
                    round_h(i)
                dve.wait_ge(h_rounded, i + 1)
                dve.tensor_tensor(hT_lo[:], hT[:], hT_hi[:].bitcast(F32), ALU.subtract).then_inc(h_split, 1)

            dve.wait_ge(x_loaded, 16)
            ln_moments_of(0, 0)
            ln_normalize(0, 0)
            dve.wait_ge(cond_exp, 1)
            dve.tensor_scalar(sigmoid_den[:], sigmoid_den[:], 1.0, None, ALU.add).then_inc(cond_chain, 1)
            dve.wait_ge(cond_chain, 1)
            dve.reciprocal(sigmoid[:], sigmoid_den[:]).then_inc(cond_chain, 1)
            dve.wait_ge(cond_chain, 2)
            dve.tensor_tensor(siluT[:], job_x[:, :, 0:B], sigmoid[:], ALU.mult).then_inc(siluT_ready, 1)

            dve.wait_ge(cols_transposed, 1)
            dve.tensor_copy(bias_cols[:], attn_ps[1][:, 0, 0:20]).then_inc(cols_ready, 1)
            dve.wait_ge(cols_ready, 1)
            dve.tensor_scalar(bias_cols[:, 0:2], bias_cols[:, 0:2], SCALE, None, ALU.mult).then_inc(bq_scaled, 1)
            dve.wait_ge(ld_qkv, 16)
            dve.tensor_scalar(wqkv_raw[:, :, 0:H], wqkv_raw[:, :, 0:H], SCALE, None, ALU.mult).then_inc(wq_scaled, 1)
            dve.wait_ge(wq_scaled, 1)
            dve.tensor_copy(wqkv_hi[:], wqkv_raw).then_inc(wqkv_rounded, 1)
            dve.wait_ge(wqkv_rounded, 1)
            dve.tensor_tensor(wqkv_lo[:], wqkv_raw, wqkv_hi[:].bitcast(F32), ALU.subtract).then_inc(wqkv_split, 1)

            def add_mod_bias(layer):
                dve.wait_ge(mod_products, layer + 1)
                m = slice(4 * layer, 4 * layer + 4)
                dve.tensor_tensor(mod[:, m], attn_ps[0][:, layer, 0:4 * B].rearrange("p (m b) -> p m b", b=B),
                                  b_ss_col[:, m].unsqueeze(2).to_broadcast([P, 4, B]), ALU.add).then_inc(mod_sum, 1)
                dve.wait_ge(mod_sum, layer + 1)
                scales = mod[:, 4 * layer:4 * layer + CT]
                dve.tensor_scalar(scales, scales, 1.0, None, ALU.add).then_inc(mod_ready, 1)

            add_mod_bias(0)
            split_h(0)
            dve.wait_ge(x_loaded, 32)
            ln_moments_of(1, 1)

            def make_bias(b):
                wait(dve, maxed, 2 * UNITS * b)
                pad = pad_keys[:, bass.ds(b, 1)].to_broadcast([P, TT, S])
                dve.scalar_tensor_tensor(bias[:], pad, -FLT_MAX, base_bias[:], ALU.mult, ALU.add).then_inc(bias_ready, 1)

            def split_qk(b, hi, lo, ps, cols, rounded, split):
                dve.wait_ge(rounded, 2 * b + 2)
                for t in range(CT):
                    dve.scalar_tensor_tensor(qk[:, lo, t], ps[:, t], cols[:, t:t + 1],
                                             qk[:, hi, t].bitcast(F32), ALU.add, ALU.subtract).then_inc(split, 1)

            def split_q(b):
                split_qk(b, Q_HI, Q_LO, job_x, b_qk_col[:, 0:CT], q_rounded, q_split)

            def split_k(b):
                split_qk(b, K_HI, K_LO, job_y, b_qk_col[:, CT:2 * CT], k_rounded, k_split)

            def evacuate_v(b):
                dve.wait_ge(v_products, b + 1)
                wait(dve, v_installed, b)
                dve.tensor_tensor(v_next[:], job_x[:], b_v_row[:].unsqueeze(1).to_broadcast([P, TT, H]),
                                  ALU.add).then_inc(v_evacuated, 1)

            def install_v(b):
                dve.wait_ge(v_evacuated, b + 1)
                wait(dve, attended, GROUPS * b)
                dve.tensor_copy(v_ones[:, :, :, 0:D], v_next[:].rearrange("p t (h d) -> p t h d", d=D)).then_inc(v_installed, 1)

            def bias_and_max(b, u):
                n = UNITS * b + u
                p, qt = u // 2, u % 2
                dve.wait_ge(scores_ready, n + 1)
                if qt == 0:
                    wait(dve, transposed, n - 6)
                dve.nop(nofuse=True)
                for k in range(2):
                    dve.tensor_tensor_reduce(out=shifted[:, u % 8, k], in0=scores_ps[qt][:, k], in1=bias[:, qt],
                                             scale=1.0, scalar=-FLT_MAX, op0=ALU.add, op1=ALU.max,
                                             accum_out=row_max[:, u, k:k + 1]).then_inc(maxed, 1)

            def normalize(b, qt):
                ps = (job_x, job_y)[qt][:].rearrange("p a b -> p (a b)").rearrange("p (h e) -> p h e", e=32)
                dve.wait_ge(o_transposed, 2 * b + qt + 1)
                dve.reciprocal(inv_sum[:, qt], ps[:, :, D]).then_inc(sums_inverted, 1)
                dve.wait_ge(sums_inverted, 2 * b + qt + 1)
                wait(dve, n_transposed, b)
                dve.tensor_tensor(attn[:, qt], ps[:, :, 0:D], inv_sum[:, qt].unsqueeze(2).to_broadcast([P, NH, D]),
                                  ALU.mult).then_inc(normalized, 1)

            def split_attn(b):
                dve.wait_ge(n_rounded, b + 1)
                dve.tensor_tensor(attnT_lo[:], job_x[:], attnT_hi[:].bitcast(F32), ALU.subtract).then_inc(n_split, 1)

            def first_residual(b):
                dve.wait_ge(proj_products, b + 1)
                dve.wait_ge(x_biased, b + 1)
                xb = tokens[:, bass.ds(b, 1)].rearrange("p o t c -> p (o t) c")
                dve.tensor_tensor(xb, job_y[:], xb, ALU.add).then_inc(x1_ready, 1)

            def split_first(t, hi, lo, ps, col, rounded, split):
                dve.wait_ge(rounded, t + 1)
                dve.scalar_tensor_tensor(qk[:, lo, t], ps, col, qk[:, hi, t].bitcast(F32),
                                         ALU.add, ALU.subtract).then_inc(split, 1)

            def split_first_q(t):
                split_first(t, Q_HI, Q_LO, scores_ps[t][:, 0], b_qk_col[:, t:t + 1], q_rounded, q_split)

            def split_first_k(t):
                split_first(t, K_HI, K_LO, trans_ps[t][:, 0], b_qk_col[:, CT + t:CT + t + 1], k_rounded, k_split)

            split_first_q(0)
            dve.wait_ge(ld_bias, 16 * 4)
            dve.tensor_tensor(base_bias[:], bias[:], base_bias[:], ALU.add).then_inc(base_ready, 1)
            split_first_k(0)
            ln_normalize(1, 1)
            split_first_q(1)
            dve.wait_ge(ld_cols, 16 * 4)
            dve.wait_ge(base_ready, 1)
            make_bias(0)
            split_first_k(1)
            evacuate_v(0)
            dve.wait_ge(v_products, 1)
            split_h(1)
            add_mod_bias(1)
            split_q(1)
            dve.wait_ge(w_split, 3)
            dve.wait_ge(bias_ready, 1)

            def split_h2(c):
                wait(dve, up_products, 4 * c)
                split_h(B + c)

            def split_gelu(c, j, g_hi, g_lo):
                dve.wait_ge(gelu_ready, 8 * c + 2 * j + 2)
                if j == 0 and g_hi is gelu_hi:
                    wait(dve, down_products, c)
                part = slice(2 * j, 2 * j + 2)
                dve.tensor_copy(g_hi[:, part], gelu[:, part]).then_inc(gelu_rounded, 1)
                dve.wait_ge(gelu_rounded, 4 * c + j + 1)
                dve.tensor_tensor(g_lo[:, part], gelu[:, part], g_hi[:, part].bitcast(F32),
                                  ALU.subtract).then_inc(gelu_split, 1)

            def batch(b, prev=True, cur=True, nxt=True, nxt2=True, chunk=None, qk=True):
                for s in range(PAIRS):
                    if cur:
                        bias_and_max(b, 2 * s)
                        bias_and_max(b, 2 * s + 1)
                    if s == 0 and not qk:
                        split_k(b + 1)
                    if s == 0 and nxt2:
                        dve.wait_ge(x_loaded, 16 * (b + 3))
                        ln_moments_of(b + 2, b + 2)
                    if s == 0 and chunk is not None:
                        dve.wait_ge(x1_ready, chunk + 1)
                        ln_moments_of(B + chunk, chunk)
                    if s == 1 and nxt and qk:
                        split_q(b + 1)
                    if s == 2 and nxt and qk:
                        split_k(b + 1)
                    if s == 2 and nxt2:
                        ln_normalize(b + 2, b + 2)
                    if s == 2 and chunk is not None:
                        ln_normalize(B + chunk, chunk)
                    if s == 3 and cur:
                        install_v(b)
                    if s == 3 and nxt:
                        evacuate_v(b + 1)
                    if s == 4 and prev:
                        normalize(b - 1, 0)
                        normalize(b - 1, 1)
                    if s == 5 and nxt2:
                        dve.wait_ge(v_products, b + 2)
                        round_h(b + 2)
                    if s == 5 and chunk == 0:
                        dve.wait_ge(v_products, B)
                        round_h(B)
                    if s == 2 and not cur:
                        ln_moments_of(B + 2, 2)
                        ln_normalize(B + 2, 2)
                    if s == 5 and not cur:
                        split_h2(1)
                    if s == 6 and prev:
                        split_attn(b - 1)
                    if s == 6 and not cur:
                        for j in range(4):
                            split_gelu(0, j, gelu_hi, gelu_lo)
                    if s == 7 and nxt2:
                        split_h(b + 2, rounded=True)
                    if s == 7 and chunk == 0:
                        split_h(B, rounded=True)
                    if s == 7 and nxt:
                        make_bias(b + 1)
                    if s == 7 and prev:
                        first_residual(b - 1)
                    if s == 7 and nxt:
                        dve.wait_ge(bias_ready, b + 2)

            batch(0, prev=False, qk=False)
            batch(1)
            with dve.Fori(2, B - 2) as b:
                batch(b)
            batch(B - 2, nxt2=False, chunk=0)
            batch(B - 1, nxt=False, nxt2=False, chunk=1)
            batch(B, cur=False, nxt=False, nxt2=False)

            def second_residual(c):
                dve.wait_ge(down_products, c + 1)
                dve.wait_ge(x1_biased, c + 1)
                wait(dve, stored, 16 * c)
                xb = tokens[:, bass.ds(c, 1)].rearrange("p o t c -> p (o t) c")
                dve.tensor_tensor(result[:], attn_ps[0][:], xb, ALU.add).then_inc(result_ready, 1)

            def mlp_chunk(c, nxt=True, nxt2=True):
                if nxt2:
                    ln_moments_of(B + c + 2, c + 2)
                if nxt:
                    split_h2(c + 1)
                if nxt2:
                    ln_normalize(B + c + 2, c + 2)
                if nxt:
                    second_residual(c - 1)
                for j in range(4):
                    split_gelu(c, j, gelu_hi if nxt else last_gelu_hi, gelu_lo if nxt else last_gelu_lo)
                if not nxt:
                    second_residual(c - 1)

            mlp_chunk(1)
            with dve.Fori(2, B - 2) as c:
                mlp_chunk(c)
            mlp_chunk(B - 2, nxt2=False)
            mlp_chunk(B - 1, nxt=False, nxt2=False)
            dve.wait_ge(x1_biased, B)
            dve.wait_ge(stored, 16 * (B - 1))
            for t in range(TT):
                dve.wait_ge(down_products, B + t)
                dve.tensor_tensor(result[:, t], last_down_ps[t][:, 0], tokens[:, B - 1, t], ALU.add).then_inc(result_ready, 1)

        @block.tensor
        def _(pe):
            def products(out, terms):
                last = None
                for n, (l_hi, l_lo, r_hi, r_lo) in enumerate(terms):
                    pe.matmul(out, l_hi, r_hi, start=(n == 0), stop=False)
                    pe.matmul(out, l_hi, r_lo, start=False, stop=False)
                    last = pe.matmul(out, l_lo, r_hi, start=False, stop=(n == len(terms) - 1))
                return last

            def transpose_x(i):
                pe.wait_ge(xhat_ready, 2 * i + 2)
                for t in range(TT):
                    for c in range(CT):
                        last = pe.transpose(job_y[:, c, t * P:(t + 1) * P], xhat[:, t, c * P:(c + 1) * P], ident[:])
                last.then_inc(x_transposed, 1)

            def qk_tiles(b, side, ps, done):
                for t in range(2):
                    cols = slice((2 * side + t) * P, (2 * side + t + 1) * P)
                    last = products(ps[:, t], [(wqkv_hi[:, c, cols], wqkv_lo[:, c, cols], hT_hi[:, c], hT_lo[:, c])
                                               for c in range(CT)])
                last.then_inc(done, 1)

            def q_tiles(b):
                pe.wait_ge(h_split, b + 1)
                wait(pe, v_evacuated, b)
                qk_tiles(b, 0, job_x, q_products)

            def k_tiles(b):
                pe.wait_ge(h_modulated, 2 * b + 2)
                qk_tiles(b, 1, job_y, k_products)

            def v_tiles(b):
                pe.wait_ge(q_split, 2 * b + 2)
                for t in range(TT):
                    rows = slice(t * P, (t + 1) * P)
                    last = products(job_x[:, t], [(hT_hi[:, c, rows], hT_lo[:, c, rows], wqkv_hi[:, c, 2 * H:3 * H],
                                                   wqkv_lo[:, c, 2 * H:3 * H]) for c in range(CT)])
                last.then_inc(v_products, 1)

            def scores(b, p, qt):
                n = UNITS * b + 2 * p + qt
                if qt == 0 and p % 4 == 0:
                    pe.wait_ge(stack_loaded[p // 4], 16 * 5 * (b + 1))
                wait(pe, maxed, 2 * (n - 1))
                for k in range(2):
                    h = 2 * p + k
                    last = pe.matmul(scores_ps[qt][:, k], stack[:, h // HALF, 0, h % HALF, qt * P:(qt + 1) * P],
                                     stack[:, h // HALF, 1, h % HALF],
                                     start=True, stop=True)
                last.then_inc(scores_ready, 1)

            def transpose_scores(b, p, kt):
                n = UNITS * b + 2 * p + kt
                if kt == 0:
                    pe.wait_ge(shift_done, n + 2)
                wait(pe, exp_done, n - 1)
                for k in range(2):
                    for qt in range(TT):
                        last = pe.transpose(trans_ps[kt][:, k, qt * P:(qt + 1) * P],
                                            shifted[:, 2 * (p % 4) + qt, k, kt * P:(kt + 1) * P], ident[:])
                last.then_inc(transposed, 1)

            def attend(b, g):
                pe.wait_ge(exp_done, UNITS * b + 4 * g + 4)
                if g == 0:
                    pe.wait_ge(v_installed, b + 1)
                if g % 2 == 0:
                    wait(pe, attn_evacuated, 2 * b - 1 + g // 2)
                for kt in range(2):
                    for k in range(4):
                        h = 4 * g + k
                        last = pe.matmul(attn_ps[g // 2][32 * k:32 * k + 32, g % 2], v_ones[:, kt, h, :],
                                         probs_t[:, 2 * ((h // 2) % 4) + kt, h % 2], start=(kt == 0), stop=(kt == 1),
                                         tile_position=(0, 32 * k))
                last.then_inc(attended, 1)

            def transpose_o(b, qt):
                if qt == 0:
                    pe.wait_ge(attn_evacuated, 2 * b + 2)
                    wait(pe, n_split, b)
                else:
                    wait(pe, x1_ready, b)
                for g in range(GROUPS):
                    last = pe.transpose((job_x, job_y)[qt][:, g // 2, (g % 2) * P:(g % 2 + 1) * P],
                                        attn_t[:, g, qt * P:(qt + 1) * P], ident[:])
                last.then_inc(o_transposed, 1)

            def transpose_attn(b):
                pe.wait_ge(normalized, 2 * b + 2)
                for t in range(TT):
                    for c in range(CT):
                        src = attn[:, t].rearrange("p h d -> p (h d)")[:, c * P:(c + 1) * P]
                        last = pe.transpose(job_x[:, c, t * P:(t + 1) * P], src, ident[:])
                last.then_inc(n_transposed, 1)

            def project(b):
                pe.wait_ge(n_split, b + 1)
                for t in range(TT):
                    rows = slice(t * P, (t + 1) * P)
                    last = products(job_y[:, t], [(attnT_hi[:, c, rows], attnT_lo[:, c, rows], wproj_hi[:, c],
                                                   wproj_lo[:, c]) for c in range(CT)])
                last.then_inc(proj_products, 1)

            pe.wait_ge(ident_ready, 1)
            pe.wait_ge(ld_cond, 16)
            for c in range(CT):
                last = pe.transpose(job_x[:, c, 0:B], cnd[:, c * P:(c + 1) * P], ident[0:B, 0:B])
            last.then_inc(cond_transposed, 1)
            transpose_x(0)
            pe.wait_ge(siluT_ready, 1)
            pe.wait_ge(ld_rows, 16 * 4)
            pe.transpose(attn_ps[1][:, 0, 0:20], bias_rows, ident[0:20, 0:20]).then_inc(cols_transposed, 1)

            def modulation(layer, loaded):
                pe.wait_ge(loaded, 16)
                for m in range(4):
                    for c in range(CT):
                        last = pe.matmul(attn_ps[0][:, layer, m * B:(m + 1) * B], wss_raw[:, layer, c, m * P:(m + 1) * P],
                                         siluT[:, c], start=(c == 0), stop=(c == CT - 1))
                last.then_inc(mod_products, 1)

            modulation(0, ld_wss1)
            pe.wait_ge(wqkv_split, 1)
            pe.wait_ge(h_split, 1)
            for t in range(CT):
                for side, ps, done in ((0, scores_ps, q_products), (1, trans_ps, k_products)):
                    cols = slice((2 * side + t) * P, (2 * side + t + 1) * P)
                    products(ps[t][:, 0], [(wqkv_hi[:, c, cols], wqkv_lo[:, c, cols], hT_hi[:, c], hT_lo[:, c])
                                           for c in range(CT)]).then_inc(
                        done if t == CT - 1 else first_products, 1)
            transpose_x(1)
            v_tiles(0)
            modulation(1, ld_wss2)
            q_tiles(1)
            k_tiles(1)
            pe.wait_ge(k_split, 2)
            pe.wait_ge(mod_sum, 2)
            pe.wait_ge(consts_ready, 1)
            pe.wait_ge(w_split, 3)

            up_ps = scores_ps + trans_ps

            def mlp_up_part(c, j):
                if j == 0:
                    pe.wait_ge(h_split, B + c + 1)
                wait(pe, gelu_ready, 8 * (c - 1) + 2 * j + 2)
                for k in range(2):
                    cols = slice((2 * j + k) * P, (2 * j + k + 1) * P)
                    last = products(up_ps[j][:, k], [(w1_hi[:, t, cols], w1_lo[:, t, cols], hT_hi[:, t], hT_lo[:, t])
                                                     for t in range(CT)])
                last.then_inc(up_products, 1)

            def batch(b, prev=True, cur=True, nxt=True, nxt2=True, chunk=None, qk=True):
                for s in range(PAIRS):
                    for half in range(2):
                        if cur:
                            scores(b, s, half)
                        if s >= 3 and cur:
                            transpose_scores(b, s - 3, half)
                        if s < 3 and prev:
                            transpose_scores(b - 1, s + 5, half)
                    if s == 1 and prev:
                        attend(b - 1, 2)
                    if s == 3 and prev:
                        attend(b - 1, 3)
                    if s == 5 and cur:
                        attend(b, 0)
                    if s == 7 and cur:
                        attend(b, 1)
                    if s == 0 and nxt and qk:
                        q_tiles(b + 1)
                    if s == 1 and nxt and qk:
                        k_tiles(b + 1)
                    if s == (2 if qk else 0) and nxt:
                        v_tiles(b + 1)
                    if s == 3 and nxt2:
                        pe.wait_ge(k_split, 2 * b + 4)
                        transpose_x(b + 2)
                    if s == 3 and chunk is not None:
                        if nxt:
                            pe.wait_ge(k_split, 2 * b + 4)
                        transpose_x(B + chunk)
                    if s == 4 and prev:
                        if nxt:
                            pe.wait_ge(v_evacuated, b + 2)
                        transpose_o(b - 1, 0)
                        if nxt2 or chunk is not None:
                            pe.wait_ge(h_modulated, 2 * b + 6)
                        transpose_o(b - 1, 1)
                    if s == 5 and prev:
                        transpose_attn(b - 1)
                    if s == 7 and prev:
                        project(b - 1)
                    if not cur:
                        if s == 0:
                            pe.wait_ge(maxed, 2 * UNITS * B)
                            mlp_up_part(0, 0)
                        if s == 1:
                            mlp_up_part(0, 1)
                        if s == 3:
                            pe.wait_ge(exp_done, UNITS * B)
                            mlp_up_part(0, 2)
                        if s == 4:
                            mlp_up_part(0, 3)
                        if s == 6:
                            mlp_up_part(1, 0)

            batch(0, prev=False, qk=False)
            batch(1)
            with pe.Fori(2, B - 2) as b:
                batch(b)
            batch(B - 2, nxt2=False, chunk=0)
            batch(B - 1, nxt=False, nxt2=False, chunk=1)
            batch(B, cur=False, nxt=False, nxt2=False)

            def mlp_up(c):
                for j in range(4):
                    mlp_up_part(c, j)

            def mlp_down_tile(t, ps, g_hi, g_lo):
                rows = slice(t * P, (t + 1) * P)
                return products(ps, [(g_hi[:, f, rows], g_lo[:, f, rows], w2_hi[:, f], w2_lo[:, f])
                                           for f in range(FT)])

            def mlp_down(c):
                wait(pe, result_ready, c)
                pe.wait_ge(gelu_split, 4 * c + 4)
                for t in range(TT):
                    last = mlp_down_tile(t, attn_ps[0][:, t], gelu_hi, gelu_lo)
                last.then_inc(down_products, 1)

            def transpose_x2(c):
                wait(pe, h_modulated, 2 * (B + c))
                transpose_x(B + c)

            for j in range(1, 4):
                mlp_up_part(1, j)
            pe.wait_ge(x1_ready, B)
            transpose_x2(2)
            pe.wait_ge(w_split, 7)
            mlp_down(0)
            with pe.Fori(2, B - 1) as c:
                mlp_up(c)
                transpose_x2(c + 1)
                mlp_down(c - 1)
            mlp_up(B - 1)
            mlp_down(B - 2)
            pe.wait_ge(gelu_split, 4 * B)
            for t in range(TT):
                mlp_down_tile(t, last_down_ps[t][:, 0], last_gelu_hi, last_gelu_lo).then_inc(down_products, 1)


_INS = ['x', 'fside_SxS_0', 'cond_1024', 'mask_SxS_ff0', 'mask_BxS_bf0', 'L0_cond_Wqkv', 'L0_cond_bqkv',
        'L0_cond_Wproj', 'L0_cond_bproj', 'L0_cond_Wss1', 'L0_cond_bss1', 'L0_cond_Wss2', 'L0_cond_bss2',
        'L0_cond_Wmlp1', 'L0_cond_bmlp1', 'L0_cond_Wmlp2', 'L0_cond_bmlp2']


def kernel(**inputs):
    import numpy as _np
    import concourse.bacc as _bacc
    from concourse import mybir as _mybir
    from concourse.bass_utils import run_bass_kernel_spmd as _run

    nc = _bacc.Bacc("TRN2", target_bir_lowering=False, num_devices=1)
    arrays, args = {}, []
    for name in _INS:
        a = _np.ascontiguousarray(inputs[name])
        arrays[f"in_{name}_dram"] = a
        args.append(nc.dram_tensor(f"in_{name}_dram", a.shape, _mybir.dt.from_np(a.dtype), kind="ExternalInput").ap())
    shape = _np.asarray(inputs['x']).shape
    args.append(nc.dram_tensor("out_0_dram", shape, _mybir.dt.float32, kind="ExternalOutput").ap())
    build_block(nc, *args)
    r = _run(nc, [arrays], core_ids=[0])
    return r.results[0]["out_0_dram"]
```
